# Optimizing a Trainium2 kernel written in Bass

```python
import numpy as np
import jax
import jax.numpy as jnp

def _softmax(x, axis=-1):
    return jax.nn.softmax(x, axis=axis)

def _gelu(x):
    return jax.nn.gelu(x, approximate=True)

def _silu(x):
    return jax.nn.silu(x)

def _sigmoid(x):
    return jax.nn.sigmoid(x)

def _layernorm(x, axis=-1, eps=1e-05):
    m = jnp.mean(x, axis=axis, keepdims=True)
    v = jnp.var(x, axis=axis, keepdims=True)
    return (x - m) / jnp.sqrt(v + eps)

def _scatter_add(tgt, idx, src, axis=0):
    return tgt.at[idx].add(src)

def _segment_sum(src, seg, n):
    return jax.ops.segment_sum(src, seg, n)
kernel_name = 'mk_flamingo_gated_d1_seqx_r8_4a3878'

def setup_inputs(seed: int=0):
    np.random.seed(seed)
    _w = jnp.asarray

    def _rec_inputs():
        import jax
        import jax.numpy as jnp
        _rk = jax.random.key(seed)
        x = -0.0002928 + 1 * jax.random.normal(jax.random.fold_in(_rk, 1), (16, 128, 128), jnp.float32)
        _lenS = 128 - jax.random.randint(jax.random.fold_in(_rk, 7), (16,), 0, max(1, 128 // 4) + 1, jnp.int32)
        _lenS2 = 128 - jax.random.randint(jax.random.fold_in(_rk, 8), (16,), 0, max(1, 128 // 4) + 1, jnp.int32)
        _ctx_1024P = jax.random.normal(jax.random.fold_in(_rk, 11), (16, 16, 128), jnp.float32)
        _ctx_1024c = jax.random.dirichlet(jax.random.fold_in(_rk, 511), 0.3 * jnp.ones((16,), jnp.float32), (16, 128))
        _ctx_1024t = jnp.einsum('bsk,bkd->bsd', _ctx_1024c, _ctx_1024P)
        _ctx_1024t = _ctx_1024t * jax.lax.rsqrt(jnp.mean(jnp.square(_ctx_1024t)) + 1e-12) * 0.953939
        ctx_1024 = -1.39393e-06 + 0.999914 * (_ctx_1024t + 0.3 * jax.random.normal(jax.random.fold_in(_rk, 611), (16, 128, 128), jnp.float32))
        _g = jax.random.normal(jax.random.fold_in(_rk, 9001), (2, 1), jnp.float32)
        _g = jnp.sign(_g) * jnp.maximum(jnp.abs(_g), 1.0) + (_g == 0) * 1.0
        g_xattn = _g[0]
        g_ffn = _g[1]
        return (x, ctx_1024, g_xattn, g_ffn)
    x, ctx_1024, g_xattn, g_ffn = _rec_inputs()

    def _L0_xattn_setup():
        import jax, jax.numpy as jnp
        import numpy as np
        D = 128
        H = 16
        HD = D // H
        SCALE = float(np.sqrt(HD))
        key = jax.random.key(seed)
        ks = jax.random.split(key, 12)
        B, T = (2, 256)
        std = 1.0 / np.sqrt(D)
        return {'query': jax.random.normal(ks[0], (B, T, D), jnp.float32), 'key_': jax.random.normal(ks[1], (B, T, D), jnp.float32), 'value': jax.random.normal(ks[2], (B, T, D), jnp.float32), 'Wq': jax.random.normal(ks[3], (D, D), jnp.float32) * std, 'bq': jax.random.normal(ks[4], (D,), jnp.float32) * std, 'Wk': jax.random.normal(ks[5], (D, D), jnp.float32) * std, 'bk': jax.random.normal(ks[6], (D,), jnp.float32) * std, 'Wv': jax.random.normal(ks[7], (D, D), jnp.float32) * std, 'bv': jax.random.normal(ks[8], (D,), jnp.float32) * std, 'Wo': jax.random.normal(ks[9], (D, D), jnp.float32) * std, 'bo': jax.random.normal(ks[10], (D,), jnp.float32) * std}
    _L0_xattn_all = _L0_xattn_setup()
    _L0_xattn_in = {k: v for k, v in _L0_xattn_all.items() if k in ('Wq', 'bq', 'Wk', 'bk', 'Wv', 'bv', 'Wo', 'bo')}
    del _L0_xattn_all

    def _L0_ffn_setup():
        import jax, jax.numpy as jnp
        import numpy as np
        B, S, D, E, K = (4, 256, 128, 8, 2)
        H = 4 * D
        key = jax.random.key(seed)
        ks = jax.random.split(key, 4)
        sc = lambda n: 1.0 / np.sqrt(n)
        return {'x': jax.random.normal(ks[0], (B, S, D), jnp.float32), 'gate_w': jax.random.normal(ks[1], (D, E), jnp.float32) * sc(D), 'gate_b': jnp.zeros((E,), jnp.float32), 'w1': jax.random.normal(ks[2], (E, D, H), jnp.float32) * sc(D), 'b1': jnp.zeros((E, H), jnp.float32), 'w2': jax.random.normal(ks[3], (E, H, D), jnp.float32) * sc(H), 'b2': jnp.zeros((E, D), jnp.float32)}
    _L0_ffn_all = _L0_ffn_setup()
    _L0_ffn_in = {k: v for k, v in _L0_ffn_all.items() if k in ('gate_w', 'gate_b', 'w1', 'b1', 'w2', 'b2')}
    del _L0_ffn_all
    return {'x': x, 'ctx_1024': ctx_1024, 'g_xattn': g_xattn, 'g_ffn': g_ffn, 'L0_xattn_Wq': _L0_xattn_in['Wq'], 'L0_xattn_bq': _L0_xattn_in['bq'], 'L0_xattn_Wk': _L0_xattn_in['Wk'], 'L0_xattn_bk': _L0_xattn_in['bk'], 'L0_xattn_Wv': _L0_xattn_in['Wv'], 'L0_xattn_bv': _L0_xattn_in['bv'], 'L0_xattn_Wo': _L0_xattn_in['Wo'], 'L0_xattn_bo': _L0_xattn_in['bo'], 'L0_ffn_gate_w': _L0_ffn_in['gate_w'], 'L0_ffn_gate_b': _L0_ffn_in['gate_b'], 'L0_ffn_w1': _L0_ffn_in['w1'], 'L0_ffn_b1': _L0_ffn_in['b1'], 'L0_ffn_w2': _L0_ffn_in['w2'], 'L0_ffn_b2': _L0_ffn_in['b2']}

def reference(x, ctx_1024, g_xattn, g_ffn, L0_xattn_Wq, L0_xattn_bq, L0_xattn_Wk, L0_xattn_bk, L0_xattn_Wv, L0_xattn_bv, L0_xattn_Wo, L0_xattn_bo, L0_ffn_gate_w, L0_ffn_gate_b, L0_ffn_w1, L0_ffn_b1, L0_ffn_w2, L0_ffn_b2):
    import jax
    import jax.numpy as jnp

    def _L0_xattn_ref(query, key_, value, Wq, bq, Wk, bk, Wv, bv, Wo, bo):
        import jax, jax.numpy as jnp
        import numpy as np
        D = 128
        H = 16
        HD = D // H
        SCALE = float(np.sqrt(HD))
        B, Tq, _ = query.shape
        Q = (query @ Wq.T + bq).reshape(B, Tq, H, HD).transpose(0, 2, 1, 3)
        K = (key_ @ Wk.T + bk).reshape(B, -1, H, HD).transpose(0, 2, 1, 3)
        V = (value @ Wv.T + bv).reshape(B, -1, H, HD).transpose(0, 2, 1, 3)
        scores = jnp.einsum('bhqd,bhkd->bhqk', Q, K) / SCALE
        attn = jax.nn.softmax(scores, axis=-1)
        ctx = jnp.einsum('bhqk,bhkd->bhqd', attn, V)
        ctx = ctx.transpose(0, 2, 1, 3).reshape(B, Tq, D)
        return ctx @ Wo.T + bo

    def _L0_ffn_ref(x, gate_w, gate_b, w1, b1, w2, b2):
        import jax, jax.numpy as jnp
        import numpy as np
        B, S, D, E, K = (4, 256, 128, 8, 2)
        H = 4 * D
        Bx, Sx, Dx = x.shape
        n_exp = w1.shape[0]
        logits = jnp.einsum('bsd,de->bse', x, gate_w) + gate_b
        scores = jax.nn.softmax(logits, axis=-1)
        topk_s, topk_i = jax.lax.top_k(scores, K)
        onehot = jax.nn.one_hot(topk_i, n_exp, dtype=scores.dtype)
        dispatch = jnp.einsum('bske,bsk->bse', onehot, topk_s)
        xf = x.reshape(-1, Dx)
        wf = dispatch.reshape(-1, n_exp)
        out = jnp.zeros_like(xf)
        for i in range(n_exp):
            wi = wf[:, i:i + 1]
            h = jax.nn.relu(xf * wi @ w1[i] + b1[i])
            y = h @ w2[i] + b2[i]
            out = jnp.where(wi > 0, y, out)
        return out.reshape(Bx, Sx, Dx)
    x = x + jnp.tanh(g_xattn[0]) * _L0_xattn_ref(_layernorm(x, axis=-1), ctx_1024, ctx_1024, L0_xattn_Wq, L0_xattn_bq, L0_xattn_Wk, L0_xattn_bk, L0_xattn_Wv, L0_xattn_bv, L0_xattn_Wo, L0_xattn_bo)
    x = x + jnp.tanh(g_ffn[0]) * _L0_ffn_ref(_layernorm(x, axis=-1), L0_ffn_gate_w, L0_ffn_gate_b, L0_ffn_w1, L0_ffn_b1, L0_ffn_w2, L0_ffn_b2)
    return x

_drawn_inputs = setup_inputs


def setup_inputs(seed=0):
    import zlib

    import numpy as np

    out = dict(_drawn_inputs(seed))
    spreads = {'L0_ffn_gate_b': (0.0, 0.1), 'L0_ffn_b1': (0.0, 0.1), 'L0_ffn_b2': (0.0, 0.1)}
    factors = {}
    for name, (base, spread) in spreads.items():
        noise = np.random.default_rng([zlib.crc32(name.encode()), seed]).standard_normal(out[name].shape)
        drawn = base * np.exp(spread * noise) if base else spread * noise
        out[name] = jnp.asarray(drawn.astype(out[name].dtype))
    for name, factor in factors.items():
        out[name] = (out[name] * factor).astype(out[name].dtype)
    return out
```

```python
import numpy as np
import concourse.bass as bass
from concourse import mybir
from contextlib import ExitStack

SEQS, QLEN, D = 16, 128, 128
HEADS, HD = 16, 8
EXPERTS, HID = 8, 512
TOKENS = SEQS * QLEN
P = 128
CHUNK = 4
CT = CHUNK * QLEN
CHUNKS = SEQS // CHUNK
PAIRS = HEADS // 2
TERMS = 6
STACK = 2 * TERMS * HD
NPART = 3
VW = HD + 1
HC = HID // P
CAP = TOKENS + P
TILES = TOKENS // P + EXPERTS - 1
RW = 2 * D + 1
WROW = HID + HC * D + HC
EPS = 1e-5
Q_TERM = [0, 0, 0, 1, 1, 2]
K_TERM = [0, 1, 2, 0, 1, 0]


def build(nc, io):
    fp32, bf16 = mybir.dt.float32, mybir.dt.bfloat16
    i32, u32 = mybir.dt.int32, mybir.dt.uint32
    ALU, ACT, AX = mybir.AluOpType, mybir.ActivationFunctionType, mybir.AxisListType
    ds = bass.ds

    parts_dram = {n: nc.dram_tensor(f"{n}_parts_dram", [2, NPART, HD * PAIRS, TOKENS], bf16, kind="Internal").ap()
                  for n in "kq"}
    rows_dram = nc.dram_tensor("rows_dram", [EXPERTS * CAP + P, RW], fp32, kind="Internal").ap()

    with ExitStack() as ctx:
        def sb(name, shape, dt=fp32):
            return ctx.enter_context(nc.sbuf_tensor(name, shape, dt))

        def sem(name):
            return ctx.enter_context(nc.semaphore(name))

        wq, wk, wv, wo, ident = (sb(n, [P, D]) for n in ("wq", "wk", "wv", "wo", "ident"))
        bq, bk = sb("bq", [P, 1]), sb("bk", [P, 1])
        bv, bo, gate_b = sb("bv", [P, D]), sb("bo", [P, D]), sb("gate_b", [P, EXPERTS])
        gate_w = sb("gate_w", [P, EXPERTS])
        gate_in = sb("gate_in", [P, 2])
        gates = sb("gates", [P, 2])
        identb = sb("identb", [P, P], bf16)
        before = sb("before", [P, P], bf16)
        onesb = sb("onesb", [P, P], bf16)
        eights = sb("eights", [P, EXPERTS])
        region = sb("region", [P, EXPERTS])
        upto = sb("upto", [P, EXPERTS, EXPERTS])
        tiles_no = sb("tiles_no", [P, TILES])
        token_no = sb("token_no", [P, SEQS], i32)
        spare = sb("spare", [P, RW])
        x = sb("x", [P, SEQS, D])
        x1 = sb("x1", [P, SEQS, D])
        ctxT = sb("ctxT", [P, TOKENS])
        stats = sb("stats", [P, CHUNK, 6])
        mv = sb("mv", [P, CHUNK, 2])
        std = sb("std", [P, CHUNK])
        rstd = sb("rstd", [P, CHUNK])
        eps = sb("eps", [P, 1])
        xn = sb("xn", [P, CHUNK, D])
        xnT = sb("xnT", [P, CT])
        proj = {n: sb(f"{n}_proj", [P, CT]) for n in "kq"}
        rest = sb("rest", [P, CT])
        part = {n: sb(f"{n}_part", [P, NPART, CT], bf16) for n in "kq"}
        qst = sb("qst", [P, PAIRS, 2, TOKENS], bf16)
        kst = sb("kst", [STACK + 2, PAIRS, TOKENS], bf16)
        vall = sb("vall", [P, SEQS, HEADS, VW])
        vcur = [sb(f"vcur{u}", [P, HEADS, VW]) for u in range(2)]
        smax = [sb(f"smax{u}", [P, HEADS]) for u in range(2)]
        nmax = [sb(f"nmax{u}", [P, 2, HEADS], bf16) for u in range(2)]
        nmaxT = [sb(f"nmaxT{u}", [2 * HEADS, P], bf16) for u in range(2)]
        probs = [sb(f"probs{u}", [P, HEADS, P]) for u in range(2)]
        oT = [sb(f"oT{u}", [P, CT]) for u in range(2)]
        rsum = sb("rsum", [P, HEADS])
        heads_out = sb("heads_out", [P, HEADS, HD])
        headsT = sb("headsT", [P, P])
        stats2 = sb("stats2", [P, SEQS, 6])
        mv2 = sb("mv2", [P, SEQS, 2])
        std2 = sb("std2", [P, SEQS])
        rstd2 = sb("rstd2", [P, SEQS])
        E3 = [P, CHUNK, EXPERTS]
        logit, escore, score, score2, hit = (sb(n, E3) for n in ("logit", "escore", "score", "score2", "hit"))
        chosen = sb("chosen", E3)
        chosenb = sb("chosenb", [P, CHUNK + 1, EXPERTS], bf16)
        r1, r2, r3, r4 = (sb(f"r{k}", [P, CHUNK]) for k in range(1, 5))
        weight = sb("weight", [P, CHUNK])
        count = sb("count", [P, EXPERTS])
        rowpos = sb("rowpos", [P, CHUNK], u32)
        routed = sb("routed", [P, CHUNK, RW])
        ntiles_i = sb("ntiles_i", [P, EXPERTS], i32)
        ntiles, ends, adjust = (sb(n, [P, EXPERTS]) for n in ("ntiles", "ends", "adjust"))
        tab8 = sb("tab8", [P, EXPERTS, EXPERTS])
        past = sb("past", [P, TILES, EXPERTS])
        past2 = sb("past2", [P, TILES, EXPERTS])
        tile_e, tile_r = sb("tile_e", [P, TILES]), sb("tile_r", [P, TILES])
        tab = sb("tab", [1, 2 * TILES + EXPERTS], i32)
        R = 4
        space, used = qst[:, :, :, :].rearrange("p g h t -> p (g h t)").bitcast(fp32), [0]

        def take(n):
            used[0] += n
            assert used[0] <= PAIRS * TOKENS
            return space[:, used[0] - n:used[0]]

        wexp = take(EXPERTS * WROW).rearrange("p (e w) -> p e w", e=EXPERTS)
        w1cur = [take(HID + HC) for u in range(R)]
        rows = [take(RW) for u in range(R)]
        rowsT = [take(P) for u in range(R)]
        hidT = [take(HC * P).rearrange("p (c t) -> p c t", c=HC) for u in range(R)]
        result = [take(D) for u in range(R)]
        tokens = [sb(f"tokens{u}", [P, 1], i32) for u in range(R)]
        b2f, b2r = sb("b2f", [P, D]), sb("b2r", [P, D])
        b2p = sb("b2p", [P, D], bf16)
        b2m = sb("b2m", [P, D], bf16)
        my_expert = sb("my_expert", [P, 1])
        pick = sb("pick", [P, TILES], bf16)

        bank = [ctx.enter_context(nc.psum_tensor(f"bank{i}", [P, CT], fp32)) for i in range(8)]

        s_w = sem("weights_loaded")
        s_xin = sem("x_loaded")
        s_cin = sem("ctx_loaded")
        s_gates = sem("gates_ready")
        s_zero = sem("stack_zeroed")
        s_ones = sem("ones_ready")
        s_spare = sem("spare_stored")
        s_var = sem("variance_ready")
        s_std = sem("std_ready")
        s_xn = sem("xn_ready")
        s_xt = sem("xn_transposed")
        s_xtc = sem("xnT_ready")
        s_proj = {n: sem(f"{n}_projected") for n in "kq"}
        s_evac = {n: sem(f"{n}_evacuated") for n in "kq"}
        s_part = {n: sem(f"{n}_parts_ready") for n in "kq"}
        s_store = {n: sem(f"{n}_parts_stored") for n in "kq"}
        s_v = sem("v_projected")
        s_vc = sem("v_ready")
        s_stack = sem("stack_loaded")
        s_chain = sem("dve_own_order")
        s_seq = sem("sequences_stacked")
        s_s1 = sem("score_quarters_ready")
        s_mx = sem("maxima_quarters_taken")
        s_nm = sem("minus_max_ready")
        s_mt = sem("max_transposed")
        s_mtc = sem("max_copied")
        s_mrow = [sem("max_rows_even"), sem("max_rows_odd")]
        s_s2 = sem("shifted_quarters_ready")
        s_exp = sem("probs_quarters_ready")
        s_vcur = sem("vcur_ready")
        s_pv = sem("pv_done")
        s_ot = sem("pv_evacuated")
        s_ott = sem("pv_transposed")
        s_norm = sem("heads_normalised")
        s_ht = sem("heads_transposed")
        s_htc = sem("headsT_ready")
        s_wo = sem("output_projected")
        s_x1 = sem("x1_ready")
        s_rs = sem("sums_inverted")
        s_nh = sem("minus_max_high_ready")
        s_var2 = sem("variances2_ready")
        s_std2 = sem("std2_ready")
        s_rxn = sem("route_xn_ready")
        s_rxt = sem("route_xn_transposed")
        s_rxtc = sem("route_xnT_ready")
        s_gate = sem("gate_product_ready")
        s_shift = sem("gate_logits_shifted")
        s_gexp = sem("gate_exp_ready")
        s_oh = sem("choice_ready")
        s_rank = sem("ranks_ready")
        s_routed = sem("routed_rows_ready")
        s_scat = sem("routed_rows_scattered")
        s_tab = sem("tile_table_ready")
        s_pad = sem("pads_stored")
        s_tile = [sem(f"tile_loaded_{u}") for u in range(R)]
        s_wexp = sem("expert_weights_loaded")
        s_w1 = sem("w1_in_place")
        s_b2 = sem("b2_split")
        s_tt = sem("rows_transposed")
        s_ttc = sem("rowsT_ready")
        s_up = sem("hidden_ready")
        s_ra = sem("relu_by_act")
        s_rv = sem("relu_by_dve")
        s_down = sem("expert_out_ready")
        s_res = sem("result_ready")
        s_out = [sem(f"result_stored_{u}") for u in range(R)]

        class Order:

            def __init__(self, eng):
                self.eng, self.n, self.base = eng, 0, 0

            def after(self, ins):
                self.n += 1
                ins.then_inc(s_chain, 1)
                self.eng.wait_ge(s_chain, self.base + self.n)

            def loop(self, i, length, since):
                self.base, self.n = since + i * length, 0

        def wait(eng, s, value):
            if not (isinstance(value, int) and value <= 0):
                eng.wait_ge(s, value)

        class Item:

            def __init__(self, n, lag, ring, i=None):
                if i is None:
                    self.no = n - lag
                    self.u, self.lap, self.no2 = self.no % ring, self.no // ring, self.no % 2
                else:
                    k = n - lag
                    self.no, self.u, self.lap, self.no2 = ring * i + k, k % ring, i + k // ring, k % 2

        def pipeline(eng, items, first, ring, one_step):
            def straight(n):
                one_step(lambda lag: Item(n, lag, ring) if 0 <= n - lag < items else None)
            for n in range(first):
                straight(n)
            with eng.Fori(0, (items - first) // ring) as i:
                for k in range(ring):
                    one_step(lambda lag: Item(first + k, lag, ring, i))
            for n in range(items, items + first):
                straight(n)

        LAG_MT, LAG_S2, LAG_PV, LAG_OUT = 1, 2, 3, 4
        LAG_UP, LAG_DOWN = 1, 2
        QUARTERS = 4
        EXPERTS_FIRST = 7
        assert (TILES - EXPERTS_FIRST) % R == 0 and EXPERTS_FIRST >= LAG_DOWN + R - 1

        def attention(eng, one_step):
            pipeline(eng, SEQS, LAG_OUT, 2, one_step)

        def experts(eng, one_step):
            pipeline(eng, TILES, EXPERTS_FIRST, R, one_step)

        def tok(b):
            return ds(b * QLEN, QLEN)

        WEIGHTS = (("wq", wq), ("wk", wk), ("wv", wv), ("wo", wo), ("ident", ident), ("bq", bq), ("bk", bk),
                   ("identb", identb), ("before", before), ("gate_w", gate_w), ("eights", eights),
                   ("region", region), ("b2f", b2f), ("my_expert", my_expert), ("tiles_no", tiles_no), ("token_no", token_no), ("spare", spare))
        ROWS = (("bv", bv), ("bo", bo), ("gate_b", gate_b))
        ALL_W = 16 * (len(WEIGHTS) + 1 + len(ROWS) + 2)
        LOADS = 2 * (TERMS + 3)

        def pads(eng, parity):
            for e in range(parity, EXPERTS, 2):
                first = eng.value_load(tab[0:1, 2 * TILES + e:2 * TILES + e + 1], min_val=0, max_val=EXPERTS * CAP)
                eng.dma_start(rows_dram[ds(first, P), :], spare[:, :]).then_inc(s_pad, 16)

        block = ctx.enter_context(nc.Block())

        @block.sync
        def _(sp):
            for c in range(CHUNKS):
                wait(sp, s_xin, 16 * c)
                sp.dma_start(x[:, CHUNK * c:CHUNK * (c + 1), :], io["x"][:, CHUNK * c:CHUNK * (c + 1), :]).then_inc(s_xin, 16)
                if c == 0:
                    for name, dst in WEIGHTS[:9]:
                        sp.dma_start(dst[:, :], io[name]).then_inc(s_w, 16)
            for c in range(CHUNKS):
                cols = ds(c * CT, CT)
                for n in "kq":
                    sp.wait_ge(s_part[n], c + 1)
                    for hp in range(2):
                        sp.dma_start(parts_dram[n][hp, :, :, cols].rearrange("s p t -> p s t"),
                                     part[n][64 * hp:64 * (hp + 1), :, :]).then_inc(s_store[n], 16)
                    sp.wait_ge(s_store[n], 32 * (c + 1))
                    if n == "q":
                        sp.wait_ge(s_zero, c + 1)
                    for hp in range(2):
                        src = parts_dram[n][hp].rearrange("s (d g) t -> (s d) g t", g=PAIRS)
                        row = hp * TERMS * HD
                        if n == "k":
                            for s0, parts in ((0, 3), (3, 2), (5, 1)):
                                sp.dma_start(kst[row + s0 * HD:row + (s0 + parts) * HD, :, cols],
                                             src[0:parts * HD, :, cols]).then_inc(s_stack, 16)
                        else:
                            for s, k in enumerate(Q_TERM):
                                sp.dma_start(qst[row + s * HD:row + (s + 1) * HD, :, hp, cols],
                                             src[k * HD:(k + 1) * HD, :, cols]).then_inc(s_stack, 16)
                sp.wait_ge(s_stack, 16 * LOADS * (c + 1))
                sp.sem_inc(s_seq, CHUNK)

            def one_step(item):
                if m := item(LAG_MT):
                    sp.wait_ge(s_mtc, m.no + 1)
                    sp.dma_start(qst[STACK:STACK + 2, :, :, tok(m.no)].rearrange("s g h t -> s (g h) t"),
                                 nmaxT[m.u][:, :]).then_inc(s_mrow[m.u], 16)
            attention(sp, one_step)

            sp.wait_ge(s_s1, QUARTERS * SEQS)
            sp.wait_ge(s_s2, QUARTERS * SEQS)
            for e in range(EXPERTS):
                sp.dma_start(wexp[:, e, :], io["wexp"][e * P:(e + 1) * P, :]).then_inc(s_wexp, 16)
            sp.wait_ge(s_tab, 1)
            pads(sp, 0)
            sp.wait_ge(s_pad, 16 * EXPERTS)
            sp.wait_ge(s_spare, 16)
            sp.wait_ge(s_scat, 16 * SEQS)

            def load(item):
                if t := item(0):
                    first = sp.value_load(tab[0:1, ds(t.no + TILES, 1)], min_val=0, max_val=EXPERTS * CAP)
                    wait(sp, s_res, t.no - R + 1)
                    sp.dma_start(rows[t.u], rows_dram[ds(first, P), :]).then_inc(s_tile[t.u], 16)
            experts(sp, load)

        @block.gpsimd
        def _(pool):
            u32z = qst[0:STACK, :, :, :].bitcast(u32)
            for c in range(CHUNKS):
                nc.gpsimd.memset(u32z[:, :, :, c * CT // 2:(c + 1) * CT // 2], 0).then_inc(s_zero, 1)
            pool.wait_ge(s_w, ALL_W)
            pool.dma_start(rows_dram[EXPERTS * CAP:EXPERTS * CAP + P, :], spare[:, :]).then_inc(s_spare, 16)
            for c in range(CHUNKS):
                pool.wait_ge(s_routed, c + 1)
                for t in range(CHUNK):
                    pool.indirect_dma_start(rows_dram, bass.IndirectOffsetOnAxis(ap=rowpos[:, t:t + 1], axis=0),
                                            routed[:, t, :], None).then_inc(s_scat, 16)
            for t in range(TILES):
                pool.wait_ge(s_res, t + 1)
                pool.indirect_dma_start(io["out"], bass.IndirectOffsetOnAxis(
                    ap=tokens[t % R][:, :].bitcast(u32), axis=0), result[t % R], None,
                    bounds_check=TOKENS - 1, oob_is_err=False).then_inc(s_out[t % R], 16)
            for u in range(R):
                pool.wait_ge(s_out[u], 16 * len(range(u, TILES, R)))

        @block.scalar
        def _(act):
            act.dma_start(ctxT[:, :], io["ctxT"]).then_inc(s_cin, 16)
            for name, dst in WEIGHTS[9:]:
                act.dma_start(dst[:, :], io[name]).then_inc(s_w, 16)
            act.dma_start(upto[:, :, :].rearrange("p a b -> p (a b)"), io["upto"]).then_inc(s_w, 16)
            for name, dst in ROWS:
                act.dma_start(dst[:, :], io[name].to_broadcast([P, dst.shape[1]])).then_inc(s_w, 16)
            for k, name in enumerate(("g_xattn", "g_ffn")):
                act.dma_start(gate_in[:, k:k + 1], io[name].to_broadcast([P, 1])).then_inc(s_w, 16)
            act.wait_ge(s_w, ALL_W)
            nc.scalar.activation(gates[:, :], gate_in[:, :], ACT.Tanh).then_inc(s_gates, 1)
            act.wait_ge(s_ones, 1)
            with act.Fori(0, CHUNKS) as c:
                act.wait_ge(s_var, c + 1)
                nc.scalar.activation(std[:, :], mv[:, :, 1], ACT.Sqrt, bias=eps[:, :]).then_inc(s_std, 1)
                act.wait_ge(s_xt, c + 1)
                act.wait_ge(s_proj["q"], c)
                nc.scalar.activation(xnT[:, :], bank[0][:, :], ACT.Copy).then_inc(s_xtc, 1)
                for n, b_, bias in (("k", 1, bk), ("q", 2, bq)):
                    act.wait_ge(s_proj[n], c + 1)
                    act.wait_ge(s_part[n], c)
                    act.wait_ge(s_store[n], 32 * c)
                    nc.scalar.activation(part[n][:, 0, :], bank[b_][:, :], ACT.Identity, bias=bias[:, :])
                    nc.scalar.activation(proj[n][:, :], bank[b_][:, :], ACT.Identity, bias=bias[:, :]).then_inc(s_evac[n], 1)

            def one_step(item):
                if m := item(LAG_MT):
                    act.wait_ge(s_mt, m.no + 1)
                    wait(act, s_mrow[m.u], 16 * m.lap)
                    nc.scalar.activation(nmaxT[m.u][:, :], bank[6][0:2 * HEADS, 0:P // 2].bitcast(bf16), ACT.Copy)\
                      .then_inc(s_mtc, 1)
                for h in range(2):
                    if s := item(LAG_S2):
                        if h == 0:
                            wait(act, s_pv, s.no - 1)
                        for t in (2 * h, 2 * h + 1):
                            act.wait_ge(s_s2, QUARTERS * s.no + t + 1)
                            nc.scalar.activation(probs[s.u][:, 4 * t:4 * t + 4, :].rearrange("p h q -> p (h q)"),
                                                 bank[2 + t % 2][:, :], ACT.Exp, scale=HD ** -0.5).then_inc(s_exp, 1)
                    if h == 0 and (o := item(LAG_OUT)):
                        act.wait_ge(s_ht, o.no + 1)
                        wait(act, s_wo, o.no)
                        nc.scalar.activation(headsT[:, :], bank[6][:, 128:256], ACT.Copy).then_inc(s_htc, 1)
                if v := item(LAG_PV):
                    act.wait_ge(s_pv, v.no + 1)
                    wait(act, s_ott, v.no - 1)
                    nc.scalar.activation(oT[v.u][:, :], bank[4][:, :], ACT.Copy).then_inc(s_ot, 1)
            attention(act, one_step)

            act.wait_ge(s_var2, 1)
            nc.scalar.activation(std2[:, :], mv2[:, :, 1], ACT.Sqrt, bias=eps[:, :]).then_inc(s_std2, 1)
            with act.Fori(0, CHUNKS) as c:
                act.wait_ge(s_rxt, c + 1)
                act.wait_ge(s_gate, c)
                nc.scalar.activation(xnT[:, :], bank[0][:, :], ACT.Copy).then_inc(s_rxtc, 1)
                act.wait_ge(s_shift, c + 1)
                nc.scalar.activation(escore[:, :, :].rearrange("p t e -> p (t e)"),
                                     logit[:, :, :].rearrange("p t e -> p (t e)"), ACT.Exp).then_inc(s_gexp, 1)

            act.wait_ge(s_tab, 1)
            pads(act, 1)

            def expert_step(item):
                if t := item(0):
                    act.wait_ge(s_tt, t.no + 1)
                    wait(act, s_up, t.no - R + 1)
                    nc.scalar.activation(rowsT[t.u], bank[0][:, 0:P], ACT.Copy).then_inc(s_ttc, 1)
                if k := item(LAG_UP):
                    act.wait_ge(s_up, k.no + 1)
                    wait(act, s_down, k.no - R + 1)
                    for c in range(2):
                        ins = nc.scalar.activation(hidT[k.u][:, c, :], bank[1 + k.no2][:, c * P:(c + 1) * P], ACT.Relu,
                                                   bias=w1cur[k.u][:, HID + c:HID + c + 1])
                    ins.then_inc(s_ra, 1)
            experts(act, expert_step)

        @block.vector
        def _(dve):
            order = Order(dve)
            V = nc.vector
            V.memset(onesb[:, :], 1.0)
            V.memset(kst[STACK:STACK + 2, :, :], 1.0)
            V.memset(vall[:, :, :, HD:VW], 1.0)
            V.memset(count[:, :], 0.0)
            V.memset(chosenb[:, CHUNK, :], 0.0)
            V.memset(bank[4][:, :], 0.0)
            V.memset(eps[:, :], EPS).then_inc(s_ones, 1)
            dve.wait_ge(s_w, ALL_W)
            L_PREP = 6
            for c in range(CHUNKS):
                order.loop(c, L_PREP, 0)
                dve.wait_ge(s_xin, 16 * c + 16)
                for t in range(CHUNK):
                    ins = V.bn_stats(stats[:, t, :], x[:, ds(CHUNK * c + t, 1), :].rearrange("p a d -> p (a d)"))
                order.after(ins)
                for t in range(CHUNK):
                    ins = V.bn_aggr(mv[:, t, :], stats[:, t, :])
                ins.then_inc(s_var, 1)
                dve.wait_ge(s_std, c + 1)
                order.after(V.reciprocal(rstd[:, :], std[:, :]))
                wait(dve, s_xt, c)
                for t in range(CHUNK):
                    ins = V.tensor_scalar(xn[:, t, :], x[:, ds(CHUNK * c + t, 1), :].rearrange("p a d -> p (a d)"),
                                          mv[:, t, 0:1], rstd[:, t:t + 1], ALU.subtract, ALU.mult)
                ins.then_inc(s_xn, 1)
                for n in "kq":
                    dve.wait_ge(s_evac[n], c + 1)
                    if n == "q":
                        dve.wait_ge(s_part["k"], c + 1)
                    elif c:
                        dve.wait_ge(s_part["q"], c)
                    order.after(V.tensor_tensor(rest[:, :], proj[n][:, :], part[n][:, 0, :], ALU.subtract))
                    order.after(V.tensor_copy(part[n][:, 1, :], rest[:, :]))
                    V.tensor_tensor(part[n][:, 2, :], rest[:, :], part[n][:, 1, :], ALU.subtract).then_inc(s_part[n], 1)
            assert order.n == L_PREP
            order.base, order.n = L_PREP * CHUNKS, 0
            dve.wait_ge(s_gates, 1)
            for c in range(CHUNKS):
                dve.wait_ge(s_v, c + 1)
                V.tensor_tensor(vall[:, CHUNK * c:CHUNK * (c + 1), :, 0:HD],
                                bank[4 + c][:, :].rearrange("p (b h d) -> p b h d", b=CHUNK, h=HEADS),
                                bv[:, :].rearrange("p (h d) -> p h d", h=HEADS).unsqueeze(1)
                                .to_broadcast([P, CHUNK, HEADS, HD]), ALU.add).then_inc(s_vc, 1)
            order.after(V.tensor_scalar(bo[:, :], bo[:, :], gates[:, 0:1], None, ALU.mult))
            order.after(V.tensor_tensor(x[:, :, :], x[:, :, :], bo[:, :].unsqueeze(1).to_broadcast([P, SEQS, D]), ALU.add))
            dve.wait_ge(s_vc, CHUNKS)
            V.memset(bank[4][:, :], 0.0).then_inc(s_vc, 1)

            parts3 = [slice(32 * k, 32 * k + EXPERTS) for k in range(NPART)]
            order.after(V.tensor_copy(b2p[:, :], b2f[:, :]))
            order.after(V.tensor_tensor(b2r[:, :], b2f[:, :], b2p[:, :], ALU.subtract))
            order.after(V.tensor_copy(b2m[:, :], b2r[:, :]))
            V.tensor_copy(b2p[parts3[1], :], b2m[parts3[1], :])
            V.tensor_tensor(b2p[parts3[2], :], b2r[parts3[2], :], b2m[parts3[2], :], ALU.subtract).then_inc(s_b2, 1)

            def one_step(item):
                if v := item(LAG_PV):
                    wait(dve, s_pv, v.no - 1)
                    V.tensor_copy(vcur[v.u][:, :, :].rearrange("p h w -> p (h w)"),
                                  vall[:, ds(v.no, 1), :, :].rearrange("p b h w -> p (b h w)")).then_inc(s_vcur, 1)
                if o := item(LAG_OUT):
                    dve.wait_ge(s_ott, o.no + 1)
                    wide = bank[5][:, :].rearrange("p (h w) -> p h w", w=32)
                    V.reciprocal(rsum[:, :], wide[:, :, HD]).then_inc(s_rs, 1)
                    dve.wait_ge(s_rs, o.no + 1)
                    wait(dve, s_ht, o.no)
                    V.tensor_tensor(heads_out[:, :, :], wide[:, :, 0:HD],
                                    rsum[:, :].unsqueeze(2).to_broadcast([P, HEADS, HD]), ALU.mult).then_inc(s_norm, 1)
                for h in range(2):
                    if m := item(0):
                        for t in (2 * h, 2 * h + 1):
                            dve.wait_ge(s_s1, QUARTERS * m.no + t + 1)
                            V.reduce_max(smax[m.u][:, 4 * t:4 * t + 4],
                                         bank[t % 2][:, :].rearrange("p (h k) -> p h k", h=4), axis=AX.X).then_inc(s_mx, 1)
                    if h == 0 and o:
                        dve.wait_ge(s_wo, o.no + 1)
                        row = ds(o.no, 1)
                        V.scalar_tensor_tensor(out=x1[:, row, :].rearrange("p a d -> p (a d)"), in0=bank[7][:, 0:D],
                                               scalar=gates[:, 0:1], in1=x[:, row, :].rearrange("p a d -> p (a d)"),
                                               op0=ALU.mult, op1=ALU.add).then_inc(s_x1, 1)
                if m:
                    wait(dve, s_mt, m.no - 1)
                    dve.wait_ge(s_mx, QUARTERS * (m.no + 1))
                    V.tensor_scalar(nmax[m.u][:, 0, :], smax[m.u][:, :], -1.0, None, ALU.mult).then_inc(s_nh, 1)
                    dve.wait_ge(s_nh, m.no + 1)
                    V.scalar_tensor_tensor(out=nmax[m.u][:, 1, :], in0=smax[m.u][:, :], scalar=-1.0,
                                           in1=nmax[m.u][:, 0, :], op0=ALU.mult, op1=ALU.subtract).then_inc(s_nm, 1)
            attention(dve, one_step)

            dve.wait_ge(s_x1, SEQS)
            for b in range(SEQS):
                ins = V.bn_stats(stats2[:, b, :], x1[:, b, :])
            order.after(ins)
            for b in range(SEQS):
                ins = V.bn_aggr(mv2[:, b, :], stats2[:, b, :])
            ins.then_inc(s_var2, 1)
            dve.wait_ge(s_std2, 1)
            order.after(V.reciprocal(rstd2[:, :], std2[:, :]))
            since, L_ROUTE = order.base + order.n, 26
            E8 = [P, CHUNK, EXPERTS]

            def wide4(a):
                return a[:, :].unsqueeze(2).to_broadcast(E8)

            def all4(a):
                return a[:, :].unsqueeze(1).to_broadcast(E8)

            with dve.Fori(0, CHUNKS) as c:
                order.loop(c, L_ROUTE, since)
                dve.wait_ge(s_rxt, c)
                dve.wait_ge(s_scat, 64 * c)
                for t in range(CHUNK):
                    b = ds(CHUNK * c + t, 1)
                    ins = V.tensor_scalar(xn[:, t, :], x1[:, b, :].rearrange("p a d -> p (a d)"),
                                          mv2[:, b, 0:1].rearrange("p a d -> p (a d)"), rstd2[:, b],
                                          ALU.subtract, ALU.mult)
                ins.then_inc(s_rxn, 1)
                V.tensor_copy(routed[:, :, 0:D], x1[:, ds(CHUNK * c, CHUNK), :])
                V.tensor_copy(routed[:, :, 2 * D:RW].bitcast(i32).rearrange("p t o -> p (t o)"),
                              token_no[:, ds(CHUNK * c, CHUNK)])
                dve.wait_ge(s_gate, c + 1)
                order.after(V.tensor_tensor(logit[:, :, :], bank[1][:, 0:CHUNK * EXPERTS].rearrange(
                    "p (t e) -> p t e", t=CHUNK), all4(gate_b), ALU.add))
                order.after(V.reduce_max(r1[:, :], logit[:, :, :], axis=AX.X))
                V.tensor_tensor(logit[:, :, :], logit[:, :, :], wide4(r1), ALU.subtract).then_inc(s_shift, 1)
                dve.wait_ge(s_gexp, c + 1)
                order.after(V.reduce_sum(r1[:, :], escore[:, :, :], axis=AX.X))
                order.after(V.reciprocal(r2[:, :], r1[:, :]))
                order.after(V.tensor_tensor(score[:, :, :], escore[:, :, :], wide4(r2), ALU.mult))
                order.after(V.reduce_max(r1[:, :], score[:, :, :], axis=AX.X))
                order.after(V.tensor_tensor(hit[:, :, :], score[:, :, :], wide4(r1), ALU.is_equal))
                order.after(V.tensor_tensor(hit[:, :, :], hit[:, :, :], all4(eights), ALU.mult))
                order.after(V.reduce_max(r2[:, :], hit[:, :, :], axis=AX.X))
                order.after(V.tensor_tensor(hit[:, :, :], all4(eights), wide4(r2), ALU.is_equal))
                order.after(V.scalar_tensor_tensor(out=score2[:, :, :], in0=hit[:, :, :], scalar=-2.0,
                                                   in1=score[:, :, :], op0=ALU.mult, op1=ALU.add))
                order.after(V.reduce_max(r3[:, :], score2[:, :, :], axis=AX.X))
                order.after(V.tensor_tensor(hit[:, :, :], score2[:, :, :], wide4(r3), ALU.is_equal))
                order.after(V.tensor_tensor(hit[:, :, :], hit[:, :, :], all4(eights), ALU.mult))
                order.after(V.reduce_max(r4[:, :], hit[:, :, :], axis=AX.X))
                order.after(V.tensor_tensor(r4[:, :], r4[:, :], r2[:, :], ALU.subtract))
                order.after(V.tensor_scalar(r4[:, :], r4[:, :], 0.0, None, ALU.min))
                order.after(V.scalar_tensor_tensor(out=r4[:, :], in0=r3[:, :], scalar=0.0, in1=r4[:, :],
                                                   op0=ALU.is_gt, op1=ALU.mult))
                order.after(V.tensor_tensor(r2[:, :], r2[:, :], r4[:, :], ALU.add))
                order.after(V.tensor_tensor(chosen[:, :, :], all4(eights), wide4(r2), ALU.is_equal))
                V.tensor_copy(chosenb[:, 0:CHUNK, :], chosen[:, :, :]).then_inc(s_oh, 1)
                order.after(V.tensor_tensor(hit[:, :, :], chosen[:, :, :], score[:, :, :], ALU.mult))
                order.after(V.reduce_sum(weight[:, :], hit[:, :, :], axis=AX.X))
                V.tensor_tensor(routed[:, :, D:2 * D], xn[:, :, :],
                                weight[:, :].unsqueeze(2).to_broadcast([P, CHUNK, D]), ALU.mult)
                dve.wait_ge(s_rank, c + 1)
                ranks = bank[2][:, 0:(CHUNK + 1) * EXPERTS].rearrange("p (t e) -> p t e", e=EXPERTS)
                order.after(V.tensor_tensor(hit[:, :, :], ranks[:, 0:CHUNK, :], all4(count), ALU.add))
                V.tensor_tensor(count[:, :], ranks[:, CHUNK, :], count[:, :], ALU.add)
                order.after(V.tensor_tensor(hit[:, :, :], hit[:, :, :], all4(region), ALU.add))
                order.after(V.tensor_tensor(hit[:, :, :], hit[:, :, :], chosen[:, :, :], ALU.mult))
                order.after(V.reduce_sum(r1[:, :], hit[:, :, :], axis=AX.X))
                V.tensor_copy(rowpos[:, :], r1[:, :]).then_inc(s_routed, 1)
            assert order.n == L_ROUTE, order.n
            order.base, order.n = since + L_ROUTE * CHUNKS, 0
            dve.wait_ge(s_routed, CHUNKS)
            order.after(V.tensor_scalar(ntiles_i[:, :], count[:, :], float(P - 1), None, ALU.add))
            order.after(V.tensor_scalar(ntiles_i[:, :], ntiles_i[:, :], 7, None, ALU.arith_shift_right))
            order.after(V.tensor_copy(ntiles[:, :], ntiles_i[:, :]))
            E88 = [P, EXPERTS, EXPERTS]
            order.after(V.tensor_tensor(tab8[:, :, :], upto[:, :, :], ntiles[:, :].unsqueeze(1).to_broadcast(E88), ALU.mult))
            order.after(V.reduce_sum(ends[:, :], tab8[:, :, :], axis=AX.X))
            ET = [P, TILES, EXPERTS]
            order.after(V.tensor_scalar(adjust[:, :], ntiles[:, :], -float(P), float(CAP), ALU.mult, ALU.add))
            order.after(V.tensor_tensor(past[:, :, :], ends[:, :].unsqueeze(1).to_broadcast(ET),
                                        tiles_no[:, :].unsqueeze(2).to_broadcast(ET), ALU.is_le))
            order.after(V.reduce_sum(tile_e[:, :], past[:, :, :], axis=AX.X))
            order.after(V.tensor_tensor(past2[:, :, :], past[:, :, :], adjust[:, :].unsqueeze(1).to_broadcast(ET), ALU.mult))
            order.after(V.reduce_sum(tile_r[:, :], past2[:, :, :], axis=AX.X))
            order.after(V.scalar_tensor_tensor(out=tile_r[:, :], in0=tiles_no[:, :], scalar=float(P), in1=tile_r[:, :],
                                               op0=ALU.mult, op1=ALU.add))
            order.after(V.tensor_scalar(tile_e[:, :], tile_e[:, :], float(EXPERTS - 1), None, ALU.min))
            V.tensor_scalar(pick[:, :], tile_e[:, :], my_expert[:, :], None, ALU.is_equal)
            V.tensor_scalar(tab[:, 0:TILES], tile_e[0:1, :], float(EXPERTS - 1), None, ALU.min)
            V.tensor_scalar(tab[:, TILES:2 * TILES], tile_r[0:1, :], float(EXPERTS * CAP), None, ALU.min)
            V.tensor_tensor(tab[:, 2 * TILES:], region[0:1, :], count[0:1, :], ALU.add).then_inc(s_tab, 1)

            dve.wait_ge(s_wexp, 16 * EXPERTS)
            dve.wait_ge(s_tab, 1)

            def expert_step(item):
                if t := item(0):
                    e = dve.value_load(tab[0:1, ds(t.no, 1)], min_val=0, max_val=EXPERTS - 1)
                    wait(dve, s_down, t.no - R + 1)
                    wait(dve, s_rv, t.no - R + 1)
                    V.tensor_copy(w1cur[t.u], wexp[:, ds(e, 1), HC * D:WROW].rearrange("p a w -> p (a w)")).then_inc(s_w1, 1)
                if k := item(LAG_UP):
                    dve.wait_ge(s_up, k.no + 1)
                    dve.wait_ge(s_w1, k.no + 1)
                    for c in range(2, HC):
                        ins = V.tensor_scalar(hidT[k.u][:, c, :], bank[3 + k.no2][:, (c - 2) * P:(c - 1) * P],
                                              w1cur[k.u][:, HID + c:HID + c + 1], 0.0, ALU.add, ALU.max)
                    ins.then_inc(s_rv, 1)
                if d := item(LAG_DOWN):
                    dve.wait_ge(s_down, d.no + 1)
                    wait(dve, s_out[d.u], 16 * d.lap)
                    V.tensor_copy(tokens[d.u][:, :], rows[d.u][:, 2 * D:RW].bitcast(i32))
                    V.scalar_tensor_tensor(out=result[d.u], in0=bank[5 + d.no2][:, 0:D], scalar=gates[:, 1:2],
                                           in1=rows[d.u][:, 0:D], op0=ALU.mult, op1=ALU.add).then_inc(s_res, 1)
            experts(dve, expert_step)

        @block.tensor
        def _(pe):
            M = nc.tensor.matmul
            pe.wait_ge(s_w, ALL_W)
            pe.wait_ge(s_cin, 16)
            pe.wait_ge(s_ones, 1)
            for b in range(SEQS):
                ins = M(bank[4 + b // CHUNK][:, (b % CHUNK) * D:(b % CHUNK + 1) * D], ctxT[:, tok(b)], wv[:, :],
                        start=True, stop=True)
                if b % CHUNK == CHUNK - 1:
                    ins.then_inc(s_v, 1)
            with pe.Fori(0, CHUNKS) as c:
                pe.wait_ge(s_evac["k"], c)
                M(bank[1][:, :], wk[:, :], ctxT[:, ds(c * CT, CT)], start=True, stop=True).then_inc(s_proj["k"], 1)
                pe.wait_ge(s_xn, c + 1)
                for t in range(CHUNK):
                    ins = nc.tensor.transpose(bank[0][:, t * P:(t + 1) * P], xn[:, t, :], ident[:, :])
                ins.then_inc(s_xt, 1)
                pe.wait_ge(s_xtc, c + 1)
                pe.wait_ge(s_evac["q"], c)
                M(bank[2][:, :], wq[:, :], xnT[:, :], start=True, stop=True).then_inc(s_proj["q"], 1)
            pe.wait_ge(s_evac["q"], CHUNKS)
            pe.wait_ge(s_vc, CHUNKS + 1)

            def one_step(item):
                if m := item(LAG_MT):
                    pe.wait_ge(s_nm, m.no + 1)
                    wait(pe, s_htc, m.no - (LAG_OUT - LAG_MT))
                    wait(pe, s_mtc, m.no)
                    nc.tensor.transpose(bank[6][0:2 * HEADS, 0:P // 2].bitcast(bf16),
                                        nmax[m.u][:, :, :].rearrange("p s h -> p (s h)"), identb[:, :]).then_inc(s_mt, 1)
                s, o, q = item(LAG_S2), item(LAG_OUT), item(0)
                for h in range(2):
                    if s:
                        if h == 0:
                            pe.wait_ge(s_mrow[s.u], 16 * (s.lap + 1))
                        for t in (2 * h, 2 * h + 1):
                            wait(pe, s_exp, QUARTERS * s.no + t - 1)
                            for k in range(2):
                                g = 2 * t + k
                                ins = M(bank[2 + t % 2][:, 256 * k:256 * (k + 1)], kst[:, g, tok(s.no)],
                                        qst[0:STACK + 2, g, :, tok(s.no)], start=True, stop=True)
                            ins.then_inc(s_s2, 1)
                    if o and h == 0:
                        pe.wait_ge(s_ot, o.no + 1)
                        wait(pe, s_norm, o.no)
                        for t in range(QUARTERS):
                            ins = nc.tensor.transpose(bank[5][:, t * P:(t + 1) * P], oT[o.u][:, t * P:(t + 1) * P], ident[:, :])
                        ins.then_inc(s_ott, 1)
                    if o and h == 1:
                        pe.wait_ge(s_htc, o.no + 1)
                        wait(pe, s_x1, o.no)
                        M(bank[7][:, 0:D], headsT[:, :], wo[:, :], start=True, stop=True).then_inc(s_wo, 1)
                    if q:
                        for t in (2 * h, 2 * h + 1):
                            if t == 0:
                                pe.wait_ge(s_seq, q.no + 1)
                            wait(pe, s_mx, QUARTERS * q.no + t - 1)
                            for k in range(4):
                                g, hp = 2 * t + k // 2, k % 2
                                ins = M(bank[t % 2][:, k * P:(k + 1) * P], qst[0:STACK, g, hp, tok(q.no)],
                                        kst[0:STACK, g, tok(q.no)], start=True, stop=True)
                            ins.then_inc(s_s1, 1)
                    if o and h == 0:
                        pe.wait_ge(s_norm, o.no + 1)
                        pe.wait_ge(s_mtc, o.no + LAG_OUT if not isinstance(o.no, int) else min(o.no + LAG_OUT, SEQS))
                        nc.tensor.transpose(bank[6][:, 128:256], heads_out[:, :, :].rearrange("p h d -> p (h d)"),
                                            ident[:, :]).then_inc(s_ht, 1)
                if v := item(LAG_PV):
                    pe.wait_ge(s_vcur, v.no + 1)
                    wait(pe, s_ot, v.no)
                    for t in range(QUARTERS):
                        pe.wait_ge(s_exp, QUARTERS * v.no + t + 1)
                        for j in range(4):
                            ins = M(bank[4][32 * j:32 * j + VW, t * P:(t + 1) * P], vcur[v.u][:, 4 * t + j, :],
                                    probs[v.u][:, 4 * t + j, :], start=True, stop=True)
                    ins.then_inc(s_pv, 1)
            attention(pe, one_step)

            with pe.Fori(0, CHUNKS) as c:
                pe.wait_ge(s_rxn, c + 1)
                pe.wait_ge(s_rxtc, c)
                for t in range(CHUNK):
                    ins = nc.tensor.transpose(bank[0][:, t * P:(t + 1) * P], xn[:, t, :], ident[:, :])
                ins.then_inc(s_rxt, 1)
                pe.wait_ge(s_rxtc, c + 1)
                pe.wait_ge(s_shift, c)
                for t in range(CHUNK):
                    ins = M(bank[1][:, t * EXPERTS:(t + 1) * EXPERTS], xnT[:, t * P:(t + 1) * P], gate_w[:, :],
                            start=True, stop=True)
                ins.then_inc(s_gate, 1)
                pe.wait_ge(s_oh, c + 1)
                pe.wait_ge(s_routed, c)
                ranks = bank[2][:, 0:(CHUNK + 1) * EXPERTS].rearrange("p (t e) -> p t e", e=EXPERTS)
                M(ranks, before[:, :], chosenb[:, :, :], start=True, stop=False)
                for t in range(CHUNK):
                    n = CHUNK - t
                    ins = M(ranks[:, t + 1:, :], onesb[:, :], chosenb[:, t:t + 1, :].to_broadcast([P, n, EXPERTS]),
                            start=False, stop=t == CHUNK - 1)
                ins.then_inc(s_rank, 1)

            pe.wait_ge(s_tab, 1)
            pe.wait_ge(s_wexp, 16 * EXPERTS)
            pe.wait_ge(s_b2, 1)

            def expert_step(item):
                if t := item(0):
                    pe.wait_ge(s_tile[t.u], 16 * (t.lap + 1))
                    wait(pe, s_ttc, t.no)
                    nc.tensor.transpose(bank[0][:, 0:P], rows[t.u][:, D:2 * D], ident[:, :]).then_inc(s_tt, 1)
                if k := item(LAG_UP):
                    pe.wait_ge(s_ttc, k.no + 1)
                    pe.wait_ge(s_w1, k.no + 1)
                    wait(pe, s_ra, k.no - 1)
                    wait(pe, s_rv, k.no - 1)
                    for c in range(HC):
                        out = bank[(1 if c < 2 else 3) + k.no2][:, c % 2 * P:(c % 2 + 1) * P]
                        ins = M(out, w1cur[k.u][:, c * P:(c + 1) * P], rowsT[k.u], start=True, stop=True)
                    ins.then_inc(s_up, 1)
                if d := item(LAG_DOWN):
                    e = pe.value_load(tab[0:1, ds(d.no, 1)], min_val=0, max_val=EXPERTS - 1)
                    wait(pe, s_res, d.no - 1)
                    out = bank[5 + d.no2][:, 0:D]
                    M(out, pick[:, ds(d.no, 1)].to_broadcast([P, P]), b2p[:, :], start=True, stop=False)
                    pe.wait_ge(s_ra, d.no + 1)
                    pe.wait_ge(s_rv, d.no + 1)
                    for c in range(HC):
                        ins = M(out, hidT[d.u][:, c, :], wexp[:, ds(e, 1), c * D:(c + 1) * D].rearrange("p a d -> p (a d)"),
                                start=False, stop=c == HC - 1)
                    ins.then_inc(s_down, 1)
            experts(pe, expert_step)


def kernel(x, ctx_1024, g_xattn, g_ffn, L0_xattn_Wq, L0_xattn_bq, L0_xattn_Wk, L0_xattn_bk, L0_xattn_Wv, L0_xattn_bv,
           L0_xattn_Wo, L0_xattn_bo, L0_ffn_gate_w, L0_ffn_gate_b, L0_ffn_w1, L0_ffn_b1, L0_ffn_w2, L0_ffn_b2):
    import concourse.bacc as bacc
    from concourse.bass_utils import run_bass_kernel_spmd
    import ml_dtypes

    a = {k: np.asarray(v) for k, v in dict(
        x=x, ctx=ctx_1024, wq=L0_xattn_Wq, bq=L0_xattn_bq, wk=L0_xattn_Wk, bk=L0_xattn_bk, wv=L0_xattn_Wv,
        bv=L0_xattn_bv, wo=L0_xattn_Wo, bo=L0_xattn_bo, gw=L0_ffn_gate_w, gb=L0_ffn_gate_b, w1=L0_ffn_w1,
        b1=L0_ffn_b1, w2=L0_ffn_w2, b2=L0_ffn_b2, gx=g_xattn, gf=g_ffn).items()}

    def by_parity(w):
        return w.reshape(PAIRS, 2, HD, -1).transpose(1, 2, 0, 3).reshape(D, -1)

    f, e = np.float32, np.arange(EXPERTS)
    spare = np.zeros((P, RW), f)
    spare[:, 2 * D] = np.full(P, TOKENS, np.int32).view(f)
    b2f, mine = np.zeros((P, D), f), np.full((P, 1), -1, f)
    for k in range(NPART):
        b2f[32 * k:32 * k + EXPERTS], mine[32 * k:32 * k + EXPERTS, 0] = a["b2"], e
    arrays = {
        "x": a["x"].transpose(1, 0, 2), "ctxT": a["ctx"].transpose(2, 0, 1).reshape(D, TOKENS),
        "wq": by_parity(a["wq"]).T, "wk": by_parity(a["wk"]).T, "wv": a["wv"].T, "wo": a["wo"].T,
        "bq": by_parity(a["bq"]), "bk": by_parity(a["bk"]), "bv": a["bv"][None], "bo": a["bo"][None],
        "g_xattn": a["gx"][None], "g_ffn": a["gf"][None], "gate_w": a["gw"], "gate_b": a["gb"][None],
        "wexp": np.concatenate([a["w2"].reshape(EXPERTS, HC, P, D).transpose(0, 2, 1, 3).reshape(EXPERTS, P, HC * D), a["w1"],
                                a["b1"].reshape(EXPERTS, HC, P).transpose(0, 2, 1)], axis=2).reshape(EXPERTS * P, WROW),
        "b2f": b2f, "my_expert": mine,
        "ident": np.eye(P, dtype=f), "identb": np.eye(P, dtype=ml_dtypes.bfloat16),
        "before": np.triu(np.ones((P, P)), 1).astype(ml_dtypes.bfloat16),
        "eights": np.tile((EXPERTS - e).astype(f), (P, 1)), "region": np.tile((e * CAP).astype(f), (P, 1)),
        "upto": np.tile((e[None, :] <= e[:, None]).astype(f).reshape(1, -1), (P, 1)),
        "tiles_no": np.tile(np.arange(TILES, dtype=f), (P, 1)),
        "token_no": (np.arange(SEQS)[None, :] * P + np.arange(P)[:, None]).astype(np.int32),
        "spare": spare,
    }
    nc = bacc.Bacc("TRN2", target_bir_lowering=False, num_devices=1)
    io, feed = {}, {}
    for name, v in arrays.items():
        v = np.ascontiguousarray(v)
        feed[f"in_{name}"] = v
        io[name] = nc.dram_tensor(f"in_{name}", v.shape, mybir.dt.from_np(v.dtype), kind="ExternalInput").ap()
    io["out"] = nc.dram_tensor("out", [TOKENS, D], mybir.dt.float32, kind="ExternalOutput").ap()
    build(nc, io)
    r = run_bass_kernel_spmd(nc, [feed], core_ids=[0])
    return r.results[0]["out"].reshape(SEQS, QLEN, D)
```

```python
import numpy as np
import concourse.bass as bass
from concourse import mybir
from contextlib import ExitStack

SEQS, QLEN, D = 16, 128, 128
HEADS, HD = 16, 8
EXPERTS, HID = 8, 512
TOKENS = SEQS * QLEN
P = 128
CHUNK = 4
CT = CHUNK * QLEN
CHUNKS = SEQS // CHUNK
PAIRS = HEADS // 2
TERMS = 6
STACK = 2 * TERMS * HD
NPART = 3
VW = HD + 1
HC = HID // P
CAP = TOKENS + P
TILES = TOKENS // P + EXPERTS - 1
RW = 2 * D + 1
WROW = HID + HC * D + HC
EPS = 1e-5
FIRST_PACK = (("wq", D), ("wk", D), ("wv", D), ("ident", P), ("bq", 1), ("bk", 1))
LATE_PACK = (("wo", D), ("gate_w", EXPERTS), ("eights", EXPERTS), ("region", EXPERTS), ("upto", EXPERTS * EXPERTS),
             ("tiles_no", TILES), ("token_no", SEQS), ("b2f", D), ("my_expert", 1), ("spare", RW))
HALF_PACK = (("identb", P), ("before", P))
ROW_PACK = (("bv", D), ("one_row", P), ("bo", D), ("gate_b", EXPERTS), ("gates", 2))
TERM_PARTS = {"q": (0, 1, 2, 0, 1, 0), "k": (0, 0, 0, 1, 1, 2)}


def build(nc, io):
    fp32, bf16 = mybir.dt.float32, mybir.dt.bfloat16
    i32, u32 = mybir.dt.int32, mybir.dt.uint32
    ALU, ACT, AX = mybir.AluOpType, mybir.ActivationFunctionType, mybir.AxisListType
    ds = bass.ds

    parts_dram = {n: nc.dram_tensor(f"{n}_parts_dram", [CHUNKS, TERMS, 2, HD, PAIRS, CT], bf16, kind="Internal").ap()
                  for n in "kq"}
    rows_dram = nc.dram_tensor("rows_dram", [EXPERTS * CAP + P, RW], fp32, kind="Internal").ap()

    with ExitStack() as ctx:
        def sb(name, shape, dt=fp32):
            return ctx.enter_context(nc.sbuf_tensor(name, shape, dt))

        def sem(name):
            return ctx.enter_context(nc.semaphore(name))

        packs = {n: sb(f"{n}_pack", [P, sum(w for _, w in fields)], dt)
                 for n, fields, dt in (("first", FIRST_PACK, fp32), ("late", LATE_PACK, fp32), ("half", HALF_PACK, bf16),
                                       ("row", ROW_PACK, fp32))}

        def field(pack, fields, name):
            at = 0
            for n, w in fields:
                if n == name:
                    return packs[pack][:, at:at + w]
                at += w

        wq, wk, wv, ident, bq, bk = (field("first", FIRST_PACK, n) for n, _ in FIRST_PACK)
        (wo, gate_w, eights, region, upto, tiles_no, token_no, b2f, my_expert, spare) = (
            field("late", LATE_PACK, n) for n, _ in LATE_PACK)
        upto = upto.rearrange("p (e f) -> p e f", e=EXPERTS)
        token_no = token_no.bitcast(i32)
        identb, before = (field("half", HALF_PACK, n) for n, _ in HALF_PACK)
        bv, one_row, bo, gate_b, gate_in = (field("row", ROW_PACK, n) for n, _ in ROW_PACK)
        gates = sb("gates", [P, 2])
        onesb = sb("onesb", [P, P], bf16)
        x = sb("x", [P, SEQS, D])
        routed = sb("routed", [P, SEQS, RW])
        x1, xn = routed[:, :, 0:D], routed[:, :, D:2 * D]
        ctxT = sb("ctxT", [P, TOKENS])
        stats = sb("stats", [P, SEQS, 6])
        mv = sb("mv", [P, SEQS, 2])
        veps = sb("veps", [P, SEQS])
        rstd = sb("rstd", [P, SEQS])
        power = sb("power", [P, SEQS])
        xnT = sb("xnT", [P, CT])
        rest = {n: sb(f"{n}_rest", [P, CT]) for n in "kq"}
        part = {n: [sb(f"{n}_part{u}", [P, NPART, CT], bf16) for u in range(2)] for n in "kq"}
        qst = sb("qst", [P, CHUNKS, 2, PAIRS, CT], bf16)
        kst = sb("kst", [STACK + 2, CHUNKS, PAIRS, CT], bf16)
        vall = sb("vall", [P, SEQS, HEADS, VW])
        smax = [sb(f"smax{u}", [P, HEADS]) for u in range(2)]
        nmax = [sb(f"nmax{u}", [P, 2, HEADS], bf16) for u in range(2)]
        nmaxT = [sb(f"nmaxT{u}", [2 * HEADS, P], bf16) for u in range(2)]
        probs = [sb(f"probs{u}", [P, HEADS, P]) for u in range(2)]
        oT = [sb(f"oT{u}", [P, CT]) for u in range(2)]
        rsum = sb("rsum", [P, HEADS])
        heads_out = sb("heads_out", [P, HEADS, HD])
        headsT = sb("headsT", [P, P])
        E3 = [P, SEQS, EXPERTS]
        logit, escore, score, score2, hit = (sb(n, E3) for n in ("logit", "escore", "score", "score2", "hit"))
        chosen = sb("chosen", E3)
        chosenb = sb("chosenb", [P, SEQS + 1, EXPERTS], bf16)
        r1, r2, r3, r4 = (sb(f"r{k}", [P, SEQS]) for k in range(1, 5))
        weight = sb("weight", [P, SEQS])
        count = sb("count", [P, EXPERTS])
        rowpos = sb("rowpos", [P, SEQS], u32)
        ntiles_i = sb("ntiles_i", [P, EXPERTS], i32)
        ntiles, ends, adjust = (sb(n, [P, EXPERTS]) for n in ("ntiles", "ends", "adjust"))
        tab8 = sb("tab8", [P, EXPERTS, EXPERTS])
        past = sb("past", [P, TILES, EXPERTS])
        past2 = sb("past2", [P, TILES, EXPERTS])
        tile_e, tile_r = sb("tile_e", [P, TILES]), sb("tile_r", [P, TILES])
        tab = sb("tab", [1, 2 * TILES + EXPERTS], i32)
        R = 6
        spaces = {"qst": qst[:, :, :, :, :].rearrange("p c h g t -> p (c h g t)").bitcast(fp32), "ctxT": ctxT[:, :]}
        used = {"qst": 0, "ctxT": 0}

        def take(n, place="qst"):
            used[place] += n
            assert used[place] <= spaces[place].shape[-1]
            return spaces[place][:, used[place] - n:used[place]]

        wexp = take(EXPERTS * WROW).rearrange("p (e w) -> p e w", e=EXPERTS)
        w1cur = [take(HID + HC) for u in range(R)]
        rows = [take(RW) for u in range(R)]
        rowsT = [take(P, "ctxT") for u in range(R)]
        hidT = [take(HC * P).rearrange("p (c t) -> p c t", c=HC) for u in range(R)]
        result = [take(D, "ctxT") for u in range(R)]
        tokens = [sb(f"tokens{u}", [P, 1], i32) for u in range(R)]
        b2r = sb("b2r", [P, D])
        b2p = sb("b2p", [P, D], bf16)
        b2m = sb("b2m", [P, D], bf16)
        pick = sb("pick", [P, TILES], bf16)

        bank = [ctx.enter_context(nc.psum_tensor(f"bank{i}", [P, CT], fp32)) for i in range(8)]

        s_w = sem("weights_loaded")
        s_xin = [sem(f"x_{c}_loaded") for c in range(CHUNKS)]
        s_cin = [sem("ctx_chunk_0_loaded"), sem("ctx_others_loaded")]
        s_gates = sem("gates_ready")
        s_zero = sem("stack_zeroed")
        s_ones = sem("ones_ready")
        s_kones = sem("k_ones_loaded")
        s_spare = sem("spare_stored")
        s_rstd = sem("rstd_ready")
        s_veps = sem("variance_plus_eps_ready")
        s_first = sem("first_weights_loaded")
        s_row = sem("row_vectors_loaded")
        s_xb = sem("x_plus_bias_ready")
        s_pool = sem("pool_own_order")
        s_xn = sem("xn_ready")
        s_xt = sem("xn_transposed")
        s_xtc = sem("xnT_ready")
        s_proj = {n: sem(f"{n}_projected") for n in "kq"}
        s_high = {n: sem(f"{n}_high_part_ready") for n in "kq"}
        s_rest = {n: sem(f"{n}_rest_ready") for n in "kq"}
        s_mid = {n: sem(f"{n}_middle_part_ready") for n in "kq"}
        s_part = {n: sem(f"{n}_parts_ready") for n in "kq"}
        s_store = {n: [sem(f"{n}_even_parts_stored"), sem(f"{n}_odd_parts_stored")] for n in "kq"}
        s_v = sem("v_projected")
        s_vc = sem("v_ready")
        s_stack = [sem(f"stack_{c}_loaded") for c in range(CHUNKS)]
        s_chain = sem("dve_own_order")
        s_s1 = sem("score_quarters_ready")
        s_mx = sem("maxima_quarters_taken")
        s_nm = sem("minus_max_ready")
        s_mt = sem("max_transposed")
        s_mtc = sem("max_copied")
        s_mrow = [sem("max_rows_even"), sem("max_rows_odd")]
        s_s2 = sem("shifted_quarters_ready")
        s_exp = sem("probs_quarters_ready")
        s_pv = sem("pv_done")
        s_ot = sem("pv_evacuated")
        s_ott = sem("pv_transposed")
        s_norm = sem("heads_normalised")
        s_ht = sem("heads_transposed")
        s_htc = sem("headsT_ready")
        s_wo = sem("output_projected")
        s_x1 = sem("x1_ready")
        s_rs = sem("sums_inverted")
        s_nh = sem("minus_max_high_ready")
        s_rxn = sem("route_xn_ready")
        s_rxt = sem("route_xn_transposed")
        s_rxtc = sem("route_xnT_ready")
        s_gate = sem("gate_product_ready")
        s_shift = sem("gate_logits_shifted")
        s_gexp = sem("gate_exp_ready")
        s_oh = sem("choice_ready")
        s_rank = sem("ranks_ready")
        s_routed = sem("routed_rows_ready")
        s_scat = sem("routed_rows_scattered")
        s_tab = sem("tile_table_ready")
        s_pad = sem("pads_stored")
        s_tile = [sem(f"tile_loaded_{u}") for u in range(R)]
        s_wexp = sem("expert_weights_loaded")
        s_w1 = sem("w1_in_place")
        s_b2 = sem("b2_split")
        s_tt = sem("rows_transposed")
        s_ttc = sem("rowsT_ready")
        s_up = sem("hidden_ready")
        s_ra = sem("relu_by_act")
        s_rv = sem("relu_by_dve")
        s_down = sem("expert_out_ready")
        s_res = sem("result_ready")
        s_out = [sem(f"result_stored_{u}") for u in range(R)]

        class Order:

            def __init__(self, eng, s):
                self.eng, self.sem, self.n, self.base = eng, s, 0, 0

            def after(self, ins):
                self.n += 1
                ins.then_inc(self.sem, 1)
                self.eng.wait_ge(self.sem, self.base + self.n)

            def loop(self, i, length, since):
                self.base, self.n = since + i * length, 0

        def wait(eng, s, value):
            if not (isinstance(value, int) and value <= 0):
                eng.wait_ge(s, value)

        class Item:

            def __init__(self, n, lag, ring, i=None):
                if i is None:
                    self.no = n - lag
                    self.u, self.lap, self.no2 = self.no % ring, self.no // ring, self.no % 2
                else:
                    k = n - lag
                    self.no, self.u, self.lap, self.no2 = ring * i + k, k % ring, i + k // ring, k % 2

        def pipeline(eng, items, first, ring, one_step, more=None):
            def straight(n):
                one_step(lambda lag: Item(n, lag, ring) if 0 <= n - lag < items else None)
            for n in range(first):
                straight(n)
            with eng.Fori(0, (items - first) // ring) as i:
                for k in range(ring):
                    one_step(lambda lag: Item(first + k, lag, ring, i))
            for n in range(items, items + first):
                straight(n)
                if more:
                    more(n - items)

        LAG_MT, LAG_S2, LAG_PV, LAG_OUT = 1, 2, 3, 4
        LAG_UP, LAG_DOWN = 1, 2
        PV_BANKS = (4, 7)
        QUARTERS = 4
        EXPERTS_FIRST = 11
        assert (TILES - EXPERTS_FIRST) % R == 0 and EXPERTS_FIRST >= LAG_DOWN + R - 1

        def attention(eng, one_step, more=None):
            pipeline(eng, SEQS, LAG_OUT, CHUNK, one_step, more)

        def attention_straight(one_step, more):
            for n in range(SEQS + LAG_OUT):
                one_step(lambda lag: Item(n, lag, CHUNK) if 0 <= n - lag < SEQS else None)
                if n >= SEQS:
                    more(n - SEQS)

        def chunk(c):
            return slice(c * CHUNK, (c + 1) * CHUNK)

        def experts(eng, one_step):
            pipeline(eng, TILES, EXPERTS_FIRST, R, one_step)

        def experts_straight(one_step):
            for n in range(TILES + LAG_DOWN):
                one_step(lambda lag: Item(n, lag, R) if 0 <= n - lag < TILES else None)

        def tok(u):
            return slice(u * QLEN, (u + 1) * QLEN)

        STORES, LOADS = 3, 4

        ALL_W = 16 * 2

        def pads(eng, parity):
            for e in range(parity, EXPERTS, 2):
                first = eng.value_load(tab[0:1, 2 * TILES + e:2 * TILES + e + 1], min_val=0, max_val=EXPERTS * CAP)
                eng.dma_start(rows_dram[ds(first, P), :], spare).then_inc(s_pad, 16)

        block = ctx.enter_context(nc.Block())

        @block.sync
        def _(sp):
            for c in range(CHUNKS):
                sp.dma_start(x[:, chunk(c), :], io["x"][:, chunk(c), :]).then_inc(s_xin[c], 16)
            sp.dma_start(kst[STACK:STACK + 2].rearrange("r c g t -> r (c g t)"), io["ones"]).then_inc(s_kones, 16)
            sp.wait_ge(s_kones, 16)
            def store(c):
                for n in "kq":
                    sp.wait_ge(s_part[n], c + 1)
                    terms = parts_dram[n][c].rearrange("s h d g t -> (h d g) s t")
                    for s0, s1 in ((0, 3), (3, 5), (5, 6)):
                        k = TERM_PARTS[n][s0:s1]
                        src = part[n][c % 2][:, k[0]:k[0] + len(set(k)), :]
                        if len(set(k)) < len(k):
                            src = src.to_broadcast([P, len(k), CT])
                        sp.dma_start(terms[:, s0:s1, :], src).then_inc(s_store[n][c % 2], 16)

            def load(c):
                for n in "kq":
                    sp.wait_ge(s_store[n][c % 2], 16 * STORES * (c // 2 + 1))
                    if n == "q":
                        sp.wait_ge(s_zero, c + 1)
                    for hp in range(2):
                        dst = kst[hp * TERMS * HD:(hp + 1) * TERMS * HD, c] if n == "k" else \
                            qst[hp * TERMS * HD:(hp + 1) * TERMS * HD, c, hp]
                        sp.dma_start(dst.rearrange("r g t -> r (g t)"),
                                     parts_dram[n][c, :, hp].rearrange("s d g t -> s d (g t)")).then_inc(s_stack[c], 16)

            store(0)
            store(1)
            load(0)
            sp.wait_ge(s_mrow[0], 16)
            load(1)
            store(2)
            sp.wait_ge(s_mrow[1], 16)
            load(2)
            store(3)
            sp.wait_ge(s_mrow[0], 2 * 16)
            load(3)

            sp.wait_ge(s_s1, QUARTERS * SEQS)
            sp.wait_ge(s_s2, QUARTERS * SEQS)
            for e in range(EXPERTS):
                sp.dma_start(wexp[:, e, :], io["wexp"][e * P:(e + 1) * P, :]).then_inc(s_wexp, 16)
            sp.wait_ge(s_tab, 1)
            pads(sp, 0)
            sp.wait_ge(s_pad, 16 * EXPERTS)
            sp.wait_ge(s_spare, 16)
            sp.wait_ge(s_scat, 16 * SEQS)

            def load_tile(item):
                if t := item(0):
                    first = sp.value_load(tab[0:1, ds(t.no + TILES, 1)], min_val=0, max_val=EXPERTS * CAP)
                    wait(sp, s_res, t.no - R + 1)
                    sp.dma_start(rows[t.u], rows_dram[ds(first, P), :]).then_inc(s_tile[t.u], 16)
            experts(sp, load_tile)

        @block.gpsimd
        def _(pool):
            order = Order(pool, s_pool)
            G = nc.gpsimd
            order.after(G.memset(power[:, :], -0.5))
            for c in range(CHUNKS + 1):
                if c < CHUNKS:
                    pool.wait_ge(s_veps, c + 1)
                    G.tensor_tensor(rstd[:, chunk(c)], veps[:, chunk(c)], power[:, chunk(c)], ALU.pow).then_inc(s_rstd, 1)
                if c:
                    G.memset(qst[0:STACK, c - 1].rearrange("r h g t -> r (h g t)").bitcast(u32), 0).then_inc(s_zero, 1)
            pool.wait_ge(s_gates, 1)
            for c in range(CHUNKS):
                pool.wait_ge(s_xin[c], 16)
            pool.wait_ge(s_xn, CHUNKS)
            order.after(G.tensor_tensor(bo, bo, gates[:, 0:1].to_broadcast([P, D]), ALU.mult))
            G.tensor_tensor(x[:, :, :], x[:, :, :], bo.unsqueeze(1).to_broadcast([P, SEQS, D]), ALU.add).then_inc(s_xb, 1)
            pool.wait_ge(s_w, ALL_W)
            pool.dma_start(rows_dram[EXPERTS * CAP:EXPERTS * CAP + P, :], spare).then_inc(s_spare, 16)
            for c in range(CHUNKS):
                pool.wait_ge(s_veps, CHUNKS + c + 1)
                G.tensor_tensor(rstd[:, chunk(c)], veps[:, chunk(c)], power[:, chunk(c)], ALU.pow).then_inc(s_rstd, 1)
            for c in range(CHUNKS):
                pool.wait_ge(s_routed, c + 1)
                for t in range(c * CHUNK, (c + 1) * CHUNK):
                    pool.indirect_dma_start(rows_dram, bass.IndirectOffsetOnAxis(ap=rowpos[:, t:t + 1], axis=0),
                                            routed[:, t, :], None).then_inc(s_scat, 16)
            for t in range(TILES):
                pool.wait_ge(s_res, t + 1)
                pool.indirect_dma_start(io["out"], bass.IndirectOffsetOnAxis(
                    ap=tokens[t % R][:, :].bitcast(u32), axis=0), result[t % R], None,
                    bounds_check=TOKENS - 1, oob_is_err=False).then_inc(s_out[t % R], 16)
            for u in range(R):
                pool.wait_ge(s_out[u], 16 * len(range(u, TILES, R)))

        @block.scalar
        def _(act):
            act.dma_start(packs["first"][:, :], io["first"]).then_inc(s_first, 16)
            act.dma_start(ctxT[:, 0:CT], io["ctxT"][:, 0:CT]).then_inc(s_cin[0], 16)
            act.dma_start(packs["row"][:, :], io["row"].to_broadcast([P, packs["row"].shape[1]])).then_inc(s_row, 16)
            act.dma_start(ctxT[:, CT:TOKENS], io["ctxT"][:, CT:TOKENS]).then_inc(s_cin[1], 16)
            act.dma_start(packs["half"][:, :], io["half"]).then_inc(s_w, 16)
            act.dma_start(packs["late"][:, :], io["late"]).then_inc(s_w, 16)
            act.wait_ge(s_row, 16)
            nc.scalar.activation(gates[:, :], gate_in, ACT.Tanh).then_inc(s_gates, 1)
            act.wait_ge(s_first, 16)
            for c in range(CHUNKS):
                act.wait_ge(s_xt, c + 1)
                wait(act, s_proj["q"], c)
                nc.scalar.activation(xnT[:, :], bank[0][:, :], ACT.Copy).then_inc(s_xtc, 1)
                for n, b_, bias in (("k", 1, bk), ("q", 2, bq)):
                    act.wait_ge(s_proj[n], c + 1)
                    wait(act, s_store[n][c % 2], 16 * STORES * (c // 2))
                    nc.scalar.activation(part[n][c % 2][:, 0, :], bank[b_][:, :], ACT.Identity, bias=bias).then_inc(s_high[n], 1)
                if c == 0:
                    act.wait_ge(s_ones, 1)
                act.wait_ge(s_v, c + 1)
                nc.scalar.activation(vall[:, chunk(c), :, 0:HD], bank[4 + c][:, :].rearrange("p (b h d) -> p b h d", b=CHUNK, h=HEADS),
                                     ACT.Copy).then_inc(s_vc, 1)
                for n in "kq":
                    act.wait_ge(s_rest[n], c + 1)
                    nc.scalar.activation(part[n][c % 2][:, 1, :], rest[n][:, :], ACT.Copy).then_inc(s_mid[n], 1)
            act.wait_ge(s_vc, CHUNKS)
            act.wait_ge(s_w, ALL_W)
            for b_ in PV_BANKS:
                nc.scalar.activation(bank[b_][:, :].rearrange("p (k d) -> p k d", k=QUARTERS),
                                     spare[:, 0:P].unsqueeze(1).to_broadcast([P, QUARTERS, P]), ACT.Copy).then_inc(s_vc, 1)

            def one_step(item):
                m, s, o = item(LAG_MT), item(LAG_S2), item(LAG_OUT)
                for t in range(QUARTERS):
                    if t == 0 and o:
                        act.wait_ge(s_pv, o.no + 1)
                        nc.scalar.activation(oT[o.no2][:, :], bank[PV_BANKS[o.no2]][:, :], ACT.Copy).then_inc(s_ot, 1)
                    if t == 1 and m:
                        act.wait_ge(s_mt, m.no + 1)
                        wait(act, s_mrow[m.no2], 16 * (m.no // 2 if isinstance(m.no, int) else 2 * m.lap + m.u // 2))
                        nc.scalar.activation(nmaxT[m.no2][:, :], bank[6][0:2 * HEADS, 0:P // 2].bitcast(bf16), ACT.Copy)\
                          .then_inc(s_mtc, 1)
                    if t == 3 and o:
                        act.wait_ge(s_ht, o.no + 1)
                        wait(act, s_wo, o.no)
                        nc.scalar.activation(headsT[:, :], bank[6][:, 128:256], ACT.Copy).then_inc(s_htc, 1)
                    if s:
                        if t == 0:
                            wait(act, s_pv, s.no - 1)
                        act.wait_ge(s_s2, QUARTERS * s.no + t + 1)
                        nc.scalar.activation(probs[s.no2][:, 4 * t:4 * t + 4, :].rearrange("p h q -> p (h q)"),
                                             bank[2 + t % 2][:, :], ACT.Exp, scale=HD ** -0.5).then_inc(s_exp, 1)
                    if t == 1 and m:
                        act.wait_ge(s_mtc, m.no + 1)
                        act.dma_start(qst[STACK:STACK + 2, ds(m.lap, 1), :, :, tok(m.u)].rearrange("s c h g t -> s (c h g) t"),
                                      nmaxT[m.no2][:, :]).then_inc(s_mrow[m.no2], 16)

            def turned(c):
                act.wait_ge(s_rxt, c + 1)
                nc.scalar.activation(ctxT[:, c * CT:(c + 1) * CT], bank[c][:, :], ACT.Copy).then_inc(s_rxtc, 1)

            def more(n):
                if n >= 2:
                    turned(n - 2)
            attention(act, one_step, more)

            turned(2)
            turned(3)
            act.wait_ge(s_shift, 1)
            nc.scalar.activation(escore[:, :, :].rearrange("p t e -> p (t e)"),
                                 logit[:, :, :].rearrange("p t e -> p (t e)"), ACT.Exp).then_inc(s_gexp, 1)

            act.wait_ge(s_tab, 1)
            pads(act, 1)

            def expert_step(item):
                if t := item(0):
                    act.wait_ge(s_tt, t.no + 1)
                    wait(act, s_up, t.no - R + 1)
                    nc.scalar.activation(rowsT[t.u], bank[0][:, 0:P], ACT.Copy).then_inc(s_ttc, 1)
                if k := item(LAG_UP):
                    act.wait_ge(s_up, k.no + 1)
                    wait(act, s_down, k.no - R + 1)
                    for c in range(2):
                        ins = nc.scalar.activation(hidT[k.u][:, c, :], bank[1 + k.no2][:, c * P:(c + 1) * P], ACT.Relu,
                                                   bias=w1cur[k.u][:, HID + c:HID + c + 1])
                    ins.then_inc(s_ra, 1)
            experts(act, expert_step)

        @block.vector
        def _(dve):
            order = Order(dve, s_chain)
            V = nc.vector
            V.memset(onesb[:, :], 1.0)
            V.memset(vall[:, :, :, HD:VW], 1.0)
            V.memset(chosenb[:, SEQS, :], 0.0).then_inc(s_ones, 1)
            dve.wait_ge(s_first, 16)
            def ln_stats(c, src):
                for b in range(c * CHUNK, (c + 1) * CHUNK):
                    ins = V.bn_stats(stats[:, b, :], src[:, b, :])
                order.after(ins)
                for b in range(c * CHUNK, (c + 1) * CHUNK):
                    ins = V.bn_aggr(mv[:, b, :], stats[:, b, :])
                order.after(ins)
                V.tensor_scalar(veps[:, chunk(c)], mv[:, chunk(c), 1], EPS, None, ALU.add).then_inc(s_veps, 1)

            def ln_rows(c, src, so_far, done):
                dve.wait_ge(s_rstd, so_far + c + 1)
                for b in range(c * CHUNK, (c + 1) * CHUNK):
                    ins = V.tensor_scalar(xn[:, b, :], src[:, b, :], mv[:, b, 0:1], rstd[:, b:b + 1], ALU.subtract, ALU.mult)
                ins.then_inc(done, 1)

            def take_rest(n, c, b_, bias):
                dve.wait_ge(s_high[n], c + 1)
                wait(dve, s_part[n], c)
                V.scalar_tensor_tensor(out=rest[n][:, :], in0=bank[b_][:, :], scalar=bias, in1=part[n][c % 2][:, 0, :],
                                       op0=ALU.add, op1=ALU.subtract).then_inc(s_rest[n], 1)

            def low_part(n, c):
                dve.wait_ge(s_mid[n], c + 1)
                V.tensor_tensor(part[n][c % 2][:, 2, :], rest[n][:, :], part[n][c % 2][:, 1, :],
                                ALU.subtract).then_inc(s_part[n], 1)

            for c in range(-2, CHUNKS):
                if c + 2 < CHUNKS:
                    dve.wait_ge(s_xin[c + 2], 16)
                    ln_stats(c + 2, x)
                if c >= 0:
                    take_rest("k", c, 1, bk)
                    take_rest("q", c, 2, bq)
                if c + 2 < CHUNKS:
                    ln_rows(c + 2, x, 0, s_xn)
                if c >= 0:
                    low_part("k", c)
                    low_part("q", c)
            dve.wait_ge(s_w, ALL_W)
            V.tensor_copy(routed[:, :, 2 * D:RW].bitcast(i32).rearrange("p t o -> p (t o)"), token_no)
            dve.wait_ge(s_gates, 1)

            def one_step(item):
                m, o = item(0), item(LAG_OUT)
                for t in range(QUARTERS):
                    if t == 2 and o:
                        dve.wait_ge(s_ott, o.no + 1)
                        wide = bank[5][:, :].rearrange("p (h w) -> p h w", w=32)
                        V.reciprocal(rsum[:, :], wide[:, :, HD]).then_inc(s_rs, 1)
                        dve.wait_ge(s_rs, o.no + 1)
                        wait(dve, s_ht, o.no)
                        V.tensor_tensor(heads_out[:, :, :], wide[:, :, 0:HD],
                                        rsum[:, :].unsqueeze(2).to_broadcast([P, HEADS, HD]), ALU.mult).then_inc(s_norm, 1)
                    if m:
                        dve.wait_ge(s_s1, QUARTERS * m.no + t + 1)
                        V.reduce_max(smax[m.no2][:, :].rearrange("p (h g) -> p g h", h=2)[:, 2 * t:2 * t + 2, :],
                                     bank[t % 2][:, :].rearrange("p (g h k) -> p g h k", g=2, h=2), axis=AX.X).then_inc(s_mx, 1)
                if m:
                    wait(dve, s_mt, m.no - 1)
                    dve.wait_ge(s_mx, QUARTERS * (m.no + 1))
                    V.tensor_scalar(nmax[m.no2][:, 0, :], smax[m.no2][:, :], -1.0, None, ALU.mult).then_inc(s_nh, 1)
                if o:
                    dve.wait_ge(s_wo, o.no + 1)
                    row = ds(o.no, 1)
                    V.scalar_tensor_tensor(out=x1[:, row, :].rearrange("p a d -> p (a d)"), in0=bank[6][:, 256:256 + D],
                                           scalar=gates[:, 0:1], in1=x[:, row, :].rearrange("p a d -> p (a d)"),
                                           op0=ALU.mult, op1=ALU.add).then_inc(s_x1, 1)
                if m:
                    dve.wait_ge(s_nh, m.no + 1)
                    V.scalar_tensor_tensor(out=nmax[m.no2][:, 1, :], in0=smax[m.no2][:, :], scalar=-1.0,
                                           in1=nmax[m.no2][:, 0, :], op0=ALU.mult, op1=ALU.subtract).then_inc(s_nm, 1)

            def more(n):
                if n < CHUNKS - 1:
                    dve.wait_ge(s_x1, CHUNK * (n + 1))
                    ln_stats(n, x1)
                if n >= 1:
                    ln_rows(n - 1, x1, CHUNKS, s_rxn)
            dve.wait_ge(s_xb, 1)
            attention(dve, one_step, more)

            dve.wait_ge(s_x1, SEQS)
            ln_stats(CHUNKS - 1, x1)
            ln_rows(CHUNKS - 1, x1, CHUNKS, s_rxn)
            parts3 = [slice(32 * k, 32 * k + EXPERTS) for k in range(NPART)]
            order.after(V.tensor_copy(b2p[:, :], b2f))
            order.after(V.tensor_tensor(b2r[:, :], b2f, b2p[:, :], ALU.subtract))
            order.after(V.tensor_copy(b2m[:, :], b2r[:, :]))
            V.tensor_copy(b2p[parts3[1], :], b2m[parts3[1], :])
            V.tensor_tensor(b2p[parts3[2], :], b2r[parts3[2], :], b2m[parts3[2], :], ALU.subtract).then_inc(s_b2, 1)

            E8 = [P, SEQS, EXPERTS]

            def wide(a):
                return a[:, :].unsqueeze(2).to_broadcast(E8)

            def all_rows(a):
                return a.unsqueeze(1).to_broadcast(E8)

            dve.wait_ge(s_gate, 1)
            order.after(V.tensor_tensor(logit[:, :, :], bank[4][:, 0:SEQS * EXPERTS].rearrange(
                "p (t e) -> p t e", t=SEQS), all_rows(gate_b), ALU.add))
            order.after(V.reduce_max(r1[:, :], logit[:, :, :], axis=AX.X))
            V.tensor_tensor(logit[:, :, :], logit[:, :, :], wide(r1), ALU.subtract).then_inc(s_shift, 1)
            dve.wait_ge(s_gexp, 1)
            order.after(V.reduce_sum(r1[:, :], escore[:, :, :], axis=AX.X))
            order.after(V.reciprocal(r2[:, :], r1[:, :]))
            order.after(V.tensor_tensor(score[:, :, :], escore[:, :, :], wide(r2), ALU.mult))
            order.after(V.reduce_max(r1[:, :], score[:, :, :], axis=AX.X))
            order.after(V.tensor_tensor(hit[:, :, :], score[:, :, :], wide(r1), ALU.is_equal))
            order.after(V.tensor_tensor(hit[:, :, :], hit[:, :, :], all_rows(eights), ALU.mult))
            order.after(V.reduce_max(r2[:, :], hit[:, :, :], axis=AX.X))
            order.after(V.tensor_tensor(hit[:, :, :], all_rows(eights), wide(r2), ALU.is_equal))
            order.after(V.scalar_tensor_tensor(out=score2[:, :, :], in0=hit[:, :, :], scalar=-2.0,
                                               in1=score[:, :, :], op0=ALU.mult, op1=ALU.add))
            order.after(V.reduce_max(r3[:, :], score2[:, :, :], axis=AX.X))
            order.after(V.tensor_tensor(hit[:, :, :], score2[:, :, :], wide(r3), ALU.is_equal))
            order.after(V.tensor_tensor(hit[:, :, :], hit[:, :, :], all_rows(eights), ALU.mult))
            order.after(V.reduce_max(r4[:, :], hit[:, :, :], axis=AX.X))
            order.after(V.tensor_tensor(r4[:, :], r4[:, :], r2[:, :], ALU.subtract))
            order.after(V.tensor_scalar(r4[:, :], r4[:, :], 0.0, None, ALU.min))
            order.after(V.scalar_tensor_tensor(out=r4[:, :], in0=r3[:, :], scalar=0.0, in1=r4[:, :],
                                               op0=ALU.is_gt, op1=ALU.mult))
            order.after(V.tensor_tensor(r2[:, :], r2[:, :], r4[:, :], ALU.add))
            order.after(V.tensor_tensor(chosen[:, :, :], all_rows(eights), wide(r2), ALU.is_equal))
            V.tensor_copy(chosenb[:, 0:SEQS, :], chosen[:, :, :]).then_inc(s_oh, 1)
            order.after(V.tensor_tensor(hit[:, :, :], chosen[:, :, :], score[:, :, :], ALU.mult))
            order.after(V.reduce_sum(weight[:, :], hit[:, :, :], axis=AX.X))

            def weigh(c):
                dve.wait_ge(s_rxt, c + 1)
                return V.tensor_tensor(xn[:, chunk(c), :], xn[:, chunk(c), :],
                                       weight[:, chunk(c)].unsqueeze(2).to_broadcast([P, CHUNK, D]), ALU.mult)

            weigh(0)
            dve.wait_ge(s_rank, 1)
            ranks = bank[4][:, 256:256 + (SEQS + 1) * EXPERTS].rearrange("p (t e) -> p t e", e=EXPERTS)
            order.after(V.tensor_tensor(hit[:, :, :], ranks[:, 0:SEQS, :], all_rows(region), ALU.add))
            V.tensor_copy(count[:, :], ranks[:, SEQS, :])
            order.after(V.tensor_tensor(hit[:, :, :], hit[:, :, :], chosen[:, :, :], ALU.mult))
            order.after(V.reduce_sum(r1[:, :], hit[:, :, :], axis=AX.X))
            V.tensor_copy(rowpos[:, :], r1[:, :]).then_inc(s_routed, 1)
            for c in range(1, CHUNKS):
                weigh(c).then_inc(s_routed, 1)
            dve.wait_ge(s_routed, CHUNKS)
            order.after(V.tensor_scalar(ntiles_i[:, :], count[:, :], float(P - 1), None, ALU.add))
            order.after(V.tensor_scalar(ntiles_i[:, :], ntiles_i[:, :], 7, None, ALU.arith_shift_right))
            order.after(V.tensor_copy(ntiles[:, :], ntiles_i[:, :]))
            E88 = [P, EXPERTS, EXPERTS]
            order.after(V.tensor_tensor(tab8[:, :, :], upto, ntiles[:, :].unsqueeze(1).to_broadcast(E88), ALU.mult))
            order.after(V.reduce_sum(ends[:, :], tab8[:, :, :], axis=AX.X))
            ET = [P, TILES, EXPERTS]
            order.after(V.tensor_scalar(adjust[:, :], ntiles[:, :], -float(P), float(CAP), ALU.mult, ALU.add))
            order.after(V.tensor_tensor(past[:, :, :], ends[:, :].unsqueeze(1).to_broadcast(ET),
                                        tiles_no.unsqueeze(2).to_broadcast(ET), ALU.is_le))
            order.after(V.reduce_sum(tile_e[:, :], past[:, :, :], axis=AX.X))
            order.after(V.tensor_tensor(past2[:, :, :], past[:, :, :], adjust[:, :].unsqueeze(1).to_broadcast(ET), ALU.mult))
            order.after(V.reduce_sum(tile_r[:, :], past2[:, :, :], axis=AX.X))
            order.after(V.scalar_tensor_tensor(out=tile_r[:, :], in0=tiles_no[:, :], scalar=float(P), in1=tile_r[:, :],
                                               op0=ALU.mult, op1=ALU.add))
            order.after(V.tensor_scalar(tile_e[:, :], tile_e[:, :], float(EXPERTS - 1), None, ALU.min))
            V.tensor_scalar(pick[:, :], tile_e[:, :], my_expert, None, ALU.is_equal)
            V.tensor_scalar(tab[:, 0:TILES], tile_e[0:1, :], float(EXPERTS - 1), None, ALU.min)
            V.tensor_scalar(tab[:, TILES:2 * TILES], tile_r[0:1, :], float(EXPERTS * CAP), None, ALU.min)
            V.tensor_tensor(tab[:, 2 * TILES:], region[0:1, :], count[0:1, :], ALU.add).then_inc(s_tab, 1)

            dve.wait_ge(s_wexp, 16 * EXPERTS)
            dve.wait_ge(s_tab, 1)

            def expert_step(item):
                if t := item(0):
                    e = dve.value_load(tab[0:1, ds(t.no, 1)], min_val=0, max_val=EXPERTS - 1)
                    wait(dve, s_down, t.no - R + 1)
                    wait(dve, s_rv, t.no - R + 1)
                    V.tensor_copy(w1cur[t.u], wexp[:, ds(e, 1), HC * D:WROW].rearrange("p a w -> p (a w)")).then_inc(s_w1, 1)
                if k := item(LAG_UP):
                    dve.wait_ge(s_up, k.no + 1)
                    dve.wait_ge(s_w1, k.no + 1)
                    for c in range(2, HC):
                        ins = V.tensor_scalar(hidT[k.u][:, c, :], bank[3 + k.no2][:, (c - 2) * P:(c - 1) * P],
                                              w1cur[k.u][:, HID + c:HID + c + 1], 0.0, ALU.add, ALU.max)
                    ins.then_inc(s_rv, 1)
                if d := item(LAG_DOWN):
                    dve.wait_ge(s_down, d.no + 1)
                    wait(dve, s_out[d.u], 16 * d.lap)
                    V.tensor_copy(tokens[d.u][:, :], rows[d.u][:, 2 * D:RW].bitcast(i32))
                    V.scalar_tensor_tensor(out=result[d.u], in0=bank[5 + d.no2][:, 0:D], scalar=gates[:, 1:2],
                                           in1=rows[d.u][:, 0:D], op0=ALU.mult, op1=ALU.add).then_inc(s_res, 1)
            experts(dve, expert_step)

        @block.tensor
        def _(pe):
            M = nc.tensor.matmul

            def at(view):
                return view.rearrange("r c t -> r (c t)")

            pe.wait_ge(s_first, 16)
            for c in range(CHUNKS):
                wait(pe, s_rest["k"], c)
                if c < 2:
                    pe.wait_ge(s_cin[c], 16)
                M(bank[1][:, :], wk, ctxT[:, c * CT:(c + 1) * CT], start=True, stop=True).then_inc(s_proj["k"], 1)
                pe.wait_ge(s_xn, c + 1)
                for t in range(CHUNK):
                    ins = nc.tensor.transpose(bank[0][:, t * P:(t + 1) * P], xn[:, c * CHUNK + t, :], ident)
                ins.then_inc(s_xt, 1)
                def values():
                    if c == 0:
                        pe.wait_ge(s_row, 16)
                    for b in range(c * CHUNK, (c + 1) * CHUNK):
                        out = bank[4 + c][:, (b % CHUNK) * D:(b % CHUNK + 1) * D]
                        M(out, ctxT[:, b * QLEN:(b + 1) * QLEN], wv, start=True, stop=False)
                        ins = M(out, one_row[0:1, :], bv[0:1, :], start=False, stop=True)
                    ins.then_inc(s_v, 1)

                if c:
                    values()
                pe.wait_ge(s_xtc, c + 1)
                wait(pe, s_rest["q"], c)
                M(bank[2][:, :], wq, xnT[:, :], start=True, stop=True).then_inc(s_proj["q"], 1)
                if not c:
                    values()
            pe.wait_ge(s_rest["q"], CHUNKS)
            pe.wait_ge(s_ones, 1)
            pe.wait_ge(s_vc, CHUNKS + 2)

            def one_step(item):
                q, m, s, v, o = (item(lag) for lag in (0, LAG_MT, LAG_S2, LAG_PV, LAG_OUT))
                for t in range(QUARTERS):
                    if q:
                        if t == 0 and q.u == 0:
                            pe.wait_ge(s_stack[q.lap], 16 * LOADS)
                        wait(pe, s_mx, QUARTERS * q.no + t - 1)
                        for k in range(4):
                            g, hp = 2 * t + k // 2, k % 2
                            ins = M(bank[t % 2][:, k * P:(k + 1) * P], at(qst[0:STACK, ds(q.lap, 1), hp, g, tok(q.u)]),
                                    at(kst[0:STACK, ds(q.lap, 1), g, tok(q.u)]), start=True, stop=True)
                        ins.then_inc(s_s1, 1)
                    if s:
                        if t == 0:
                            pe.wait_ge(s_mrow[s.no2], 16 * ((s.no // 2 if isinstance(s.no, int) else 2 * s.lap + s.u // 2) + 1))
                        wait(pe, s_exp, QUARTERS * s.no + t - 1)
                        for k in range(2):
                            g = 2 * t + k
                            ins = M(bank[2 + t % 2][:, 256 * k:256 * (k + 1)], at(kst[:, ds(s.lap, 1), g, tok(s.u)]),
                                    qst[0:STACK + 2, ds(s.lap, 1), :, g, tok(s.u)].rearrange("r c h t -> r (c h) t"),
                                    start=True, stop=True)
                        ins.then_inc(s_s2, 1)
                    if v:
                        if t == 0:
                            wait(pe, s_ot, v.no - 1)
                        pe.wait_ge(s_exp, QUARTERS * v.no + t + 1)
                        for j in range(4):
                            ins = M(bank[PV_BANKS[v.no2]][32 * j:32 * j + VW, t * P:(t + 1) * P],
                                    vall[:, v.no, 4 * t + j, :], probs[v.no2][:, 4 * t + j, :], start=True, stop=True)
                        if t == QUARTERS - 1:
                            ins.then_inc(s_pv, 1)
                    if t == 0 and m:
                        pe.wait_ge(s_nm, m.no + 1)
                        wait(pe, s_x1, m.no - (LAG_OUT - LAG_MT))
                        wait(pe, s_mtc, m.no)
                        nc.tensor.transpose(bank[6][0:2 * HEADS, 0:P // 2].bitcast(bf16),
                                            nmax[m.no2][:, :, :].rearrange("p s h -> p (s h)"), identb).then_inc(s_mt, 1)
                    if t == 1 and o:
                        pe.wait_ge(s_ot, o.no + 1)
                        wait(pe, s_norm, o.no)
                        for k in range(QUARTERS):
                            ins = nc.tensor.transpose(bank[5][:, k * P:(k + 1) * P], oT[o.no2][:, k * P:(k + 1) * P], ident)
                        ins.then_inc(s_ott, 1)
                    if t == 2 and o:
                        pe.wait_ge(s_norm, o.no + 1)
                        pe.wait_ge(s_mtc, min(o.no + LAG_OUT, SEQS))
                        nc.tensor.transpose(bank[6][:, 128:256], heads_out[:, :, :].rearrange("p h d -> p (h d)"),
                                            ident).then_inc(s_ht, 1)
                    if t == 3 and o:
                        pe.wait_ge(s_htc, o.no + 1)
                        M(bank[6][:, 256:256 + D], headsT[:, :], wo, start=True, stop=True).then_inc(s_wo, 1)

            def turn(c):
                pe.wait_ge(s_rxn, c + 1)
                for t in range(CHUNK):
                    ins = nc.tensor.transpose(bank[c][:, t * P:(t + 1) * P], xn[:, c * CHUNK + t, :], ident)
                ins.then_inc(s_rxt, 1)

            def more(n):
                if n >= 2:
                    turn(n - 2)
            attention_straight(one_step, more)

            def gate(c):
                pe.wait_ge(s_rxtc, c + 1)
                for b in range(c * CHUNK, (c + 1) * CHUNK):
                    ins = M(bank[4][:, b * EXPERTS:(b + 1) * EXPERTS], ctxT[:, b * P:(b + 1) * P], gate_w,
                            start=True, stop=True)
                return ins

            pe.wait_ge(s_ot, SEQS)
            gate(0)
            turn(2)
            gate(1)
            gate(2)
            turn(3)
            ins = gate(3)
            ins.then_inc(s_gate, 1)
            pe.wait_ge(s_oh, 1)
            ranks = bank[4][:, 256:256 + (SEQS + 1) * EXPERTS].rearrange("p (t e) -> p t e", e=EXPERTS)
            M(ranks, before, chosenb[:, :, :], start=True, stop=False)
            for t in range(SEQS):
                n = SEQS - t
                ins = M(ranks[:, t + 1:, :], onesb[:, :], chosenb[:, t:t + 1, :].to_broadcast([P, n, EXPERTS]),
                        start=False, stop=t == SEQS - 1)
            ins.then_inc(s_rank, 1)

            pe.wait_ge(s_tab, 1)
            pe.wait_ge(s_wexp, 16 * EXPERTS)
            pe.wait_ge(s_b2, 1)

            def expert_step(item):
                if t := item(0):
                    pe.wait_ge(s_tile[t.u], 16 * (t.lap + 1))
                    wait(pe, s_ttc, t.no)
                    nc.tensor.transpose(bank[0][:, 0:P], rows[t.u][:, D:2 * D], ident).then_inc(s_tt, 1)
                if k := item(LAG_UP):
                    pe.wait_ge(s_ttc, k.no + 1)
                    pe.wait_ge(s_w1, k.no + 1)
                    wait(pe, s_ra, k.no - 1)
                    wait(pe, s_rv, k.no - 1)
                    for c in range(HC):
                        out = bank[(1 if c < 2 else 3) + k.no2][:, c % 2 * P:(c % 2 + 1) * P]
                        ins = M(out, w1cur[k.u][:, c * P:(c + 1) * P], rowsT[k.u], start=True, stop=True)
                    ins.then_inc(s_up, 1)
                if d := item(LAG_DOWN):
                    e = pe.value_load(tab[0:1, ds(d.no, 1)], min_val=0, max_val=EXPERTS - 1)
                    wait(pe, s_res, d.no - 1)
                    out = bank[5 + d.no2][:, 0:D]
                    M(out, pick[:, ds(d.no, 1)].to_broadcast([P, P]), b2p[:, :], start=True, stop=False)
                    pe.wait_ge(s_ra, d.no + 1)
                    pe.wait_ge(s_rv, d.no + 1)
                    for c in range(HC):
                        ins = M(out, hidT[d.u][:, c, :], wexp[:, ds(e, 1), c * D:(c + 1) * D].rearrange("p a d -> p (a d)"),
                                start=False, stop=c == HC - 1)
                    ins.then_inc(s_down, 1)
            experts_straight(expert_step)


def kernel(x, ctx_1024, g_xattn, g_ffn, L0_xattn_Wq, L0_xattn_bq, L0_xattn_Wk, L0_xattn_bk, L0_xattn_Wv, L0_xattn_bv,
           L0_xattn_Wo, L0_xattn_bo, L0_ffn_gate_w, L0_ffn_gate_b, L0_ffn_w1, L0_ffn_b1, L0_ffn_w2, L0_ffn_b2):
    import concourse.bacc as bacc
    from concourse.bass_utils import run_bass_kernel_spmd
    import ml_dtypes

    a = {k: np.asarray(v) for k, v in dict(
        x=x, ctx=ctx_1024, wq=L0_xattn_Wq, bq=L0_xattn_bq, wk=L0_xattn_Wk, bk=L0_xattn_bk, wv=L0_xattn_Wv,
        bv=L0_xattn_bv, wo=L0_xattn_Wo, bo=L0_xattn_bo, gw=L0_ffn_gate_w, gb=L0_ffn_gate_b, w1=L0_ffn_w1,
        b1=L0_ffn_b1, w2=L0_ffn_w2, b2=L0_ffn_b2, gx=g_xattn, gf=g_ffn).items()}

    def by_parity(w):
        return w.reshape(PAIRS, 2, HD, -1).transpose(1, 2, 0, 3).reshape(D, -1)

    f, e = np.float32, np.arange(EXPERTS)
    spare = np.zeros((P, RW), f)
    spare[:, 2 * D] = np.full(P, TOKENS, np.int32).view(f)
    b2f, mine = np.zeros((P, D), f), np.full((P, 1), -1, f)
    for k in range(NPART):
        b2f[32 * k:32 * k + EXPERTS], mine[32 * k:32 * k + EXPERTS, 0] = a["b2"], e
    values = {
        "wq": by_parity(a["wq"]).T, "wk": by_parity(a["wk"]).T, "wv": a["wv"].T, "wo": a["wo"].T,
        "bq": by_parity(a["bq"]), "bk": by_parity(a["bk"]), "bv": a["bv"][None], "one_row": np.ones((1, P), f), "bo": a["bo"][None],
        "gates": np.concatenate([a["gx"], a["gf"]])[None], "gate_w": a["gw"], "gate_b": a["gb"][None],
        "b2f": b2f, "my_expert": mine, "ident": np.eye(P, dtype=f), "identb": np.eye(P, dtype=ml_dtypes.bfloat16),
        "before": np.triu(np.ones((P, P)), 1).astype(ml_dtypes.bfloat16),
        "eights": np.tile((EXPERTS - e).astype(f), (P, 1)), "region": np.tile((e * CAP).astype(f), (P, 1)),
        "upto": np.tile((e[None, :] <= e[:, None]).astype(f).reshape(1, -1), (P, 1)),
        "tiles_no": np.tile(np.arange(TILES, dtype=f), (P, 1)),
        "token_no": (np.arange(SEQS)[None, :] * P + np.arange(P)[:, None]).astype(np.int32).view(f),
        "spare": spare,
    }
    arrays = {
        **{n: np.concatenate([values[k] for k, _ in fields], axis=1)
           for n, fields in (("first", FIRST_PACK), ("late", LATE_PACK), ("half", HALF_PACK), ("row", ROW_PACK))},
        "ones": np.ones((2, PAIRS * TOKENS), ml_dtypes.bfloat16),
        "x": a["x"].transpose(1, 0, 2), "ctxT": a["ctx"].transpose(2, 0, 1).reshape(D, TOKENS),
        "wexp": np.concatenate([a["w2"].reshape(EXPERTS, HC, P, D).transpose(0, 2, 1, 3).reshape(EXPERTS, P, HC * D), a["w1"],
                                a["b1"].reshape(EXPERTS, HC, P).transpose(0, 2, 1)], axis=2).reshape(EXPERTS * P, WROW),
    }
    nc = bacc.Bacc("TRN2", target_bir_lowering=False, num_devices=1)
    io, feed = {}, {}
    for name, v in arrays.items():
        v = np.ascontiguousarray(v)
        feed[f"in_{name}"] = v
        io[name] = nc.dram_tensor(f"in_{name}", v.shape, mybir.dt.from_np(v.dtype), kind="ExternalInput").ap()
    io["out"] = nc.dram_tensor("out", [TOKENS, D], mybir.dt.float32, kind="ExternalOutput").ap()
    build(nc, io)
    r = run_bass_kernel_spmd(nc, [feed], core_ids=[0])
    return r.results[0]["out"].reshape(SEQS, QLEN, D)
```

```python
import numpy as np
import concourse.bass as bass
from concourse import mybir
from contextlib import ExitStack

SEQS, QLEN, D = 16, 128, 128
HEADS, HD = 16, 8
EXPERTS, HID = 8, 512
TOKENS = SEQS * QLEN
P = 128
CHUNK = 4
CT = CHUNK * QLEN
CHUNKS = SEQS // CHUNK
HALF = SEQS // 2
PAIRS = HEADS // 2
TERMS = 6
STACK = 2 * TERMS * HD
NPART = 3
VW = HD + 1
HC = HID // P
CAP = TOKENS + P
TILES = TOKENS // P + EXPERTS - 1
RW = 2 * D + 1
WROW = HID + HC * D + HC
EPS = 1e-5
FIRST_PACK = (("wq", D), ("wk", D), ("wv", D), ("ident", P), ("bq", 1), ("bk", 1))
LATE_PACK = (("wo", D), ("gate_w", EXPERTS), ("eights", EXPERTS), ("region", EXPERTS), ("upto", EXPERTS * EXPERTS),
             ("tiles_no", TILES), ("token_no", SEQS), ("b2f", D), ("my_expert", 1), ("spare", RW))
HALF_PACK = (("identb", P), ("before", P))
ROW_PACK = (("bv", D), ("one_row", P), ("bo", D), ("gate_b", EXPERTS), ("gates", 2))
TERM_PARTS = {"q": (0, 1, 2, 0, 1, 0), "k": (0, 0, 0, 1, 1, 2)}


def build(nc, io):
    fp32, bf16 = mybir.dt.float32, mybir.dt.bfloat16
    i32, u32 = mybir.dt.int32, mybir.dt.uint32
    ALU, ACT, AX = mybir.AluOpType, mybir.ActivationFunctionType, mybir.AxisListType
    ds = bass.ds

    parts_dram = {n: nc.dram_tensor(f"{n}_parts_dram", [CHUNKS, TERMS, 2, HD, PAIRS, CT], bf16, kind="Internal").ap()
                  for n in "kq"}
    rows_dram = nc.dram_tensor("rows_dram", [EXPERTS * CAP + P, RW], fp32, kind="Internal").ap()

    with ExitStack() as ctx:
        def sb(name, shape, dt=fp32):
            return ctx.enter_context(nc.sbuf_tensor(name, shape, dt))

        def sem(name):
            return ctx.enter_context(nc.semaphore(name))

        packs = {n: sb(f"{n}_pack", [P, sum(w for _, w in fields)], dt)
                 for n, fields, dt in (("first", FIRST_PACK, fp32), ("late", LATE_PACK, fp32), ("half", HALF_PACK, bf16),
                                       ("row", ROW_PACK, fp32))}

        def field(pack, fields, name):
            at = 0
            for n, w in fields:
                if n == name:
                    return packs[pack][:, at:at + w]
                at += w

        wq, wk, wv, ident, bq, bk = (field("first", FIRST_PACK, n) for n, _ in FIRST_PACK)
        (wo, gate_w, eights, region, upto, tiles_no, token_no, b2f, my_expert, spare) = (
            field("late", LATE_PACK, n) for n, _ in LATE_PACK)
        upto = upto.rearrange("p (e f) -> p e f", e=EXPERTS)
        token_no = token_no.bitcast(i32)
        identb, before = (field("half", HALF_PACK, n) for n, _ in HALF_PACK)
        bv, one_row, bo, gate_b, gate_in = (field("row", ROW_PACK, n) for n, _ in ROW_PACK)
        gates = sb("gates", [P, 2])
        onesb = sb("onesb", [P, P], bf16)
        x = sb("x", [P, SEQS, D])
        routed = sb("routed", [P, SEQS, RW])
        x1, xn = routed[:, :, 0:D], routed[:, :, D:2 * D]
        ctxT = sb("ctxT", [P, TOKENS])
        stats = sb("stats", [P, SEQS, 6])
        mv = sb("mv", [P, SEQS, 2])
        veps = sb("veps", [P, SEQS])
        rstd = sb("rstd", [P, SEQS])
        power = sb("power", [P, SEQS])
        xnT = sb("xnT", [P, CT])
        rest = {n: sb(f"{n}_rest", [P, CT]) for n in "kq"}
        part = {n: [sb(f"{n}_part{u}", [P, NPART, CT], bf16) for u in range(2)] for n in "kq"}
        qst = sb("qst", [P, CHUNKS, 2, PAIRS, CT], bf16)
        kst = sb("kst", [STACK + 2, CHUNKS, PAIRS, CT], bf16)
        vall = sb("vall", [P, SEQS, HEADS, VW])
        smax = [sb(f"smax{u}", [P, HEADS]) for u in range(2)]
        nmax = [sb(f"nmax{u}", [P, 2, HEADS], bf16) for u in range(2)]
        nmaxT = [sb(f"nmaxT{u}", [2 * HEADS, P], bf16) for u in range(2)]
        probs = [sb(f"probs{u}", [P, HEADS, P]) for u in range(2)]
        oT = [sb(f"oT{u}", [P, CT]) for u in range(2)]
        rsum = sb("rsum", [P, HEADS])
        heads_out = sb("heads_out", [P, HEADS, HD])
        headsT = sb("headsT", [P, P])
        E3 = [P, SEQS, EXPERTS]
        logit, escore, score, score2, hit = (sb(n, E3) for n in ("logit", "escore", "score", "score2", "hit"))
        chosen = sb("chosen", E3)
        chosenb = sb("chosenb", [P, SEQS + 1, EXPERTS], bf16)
        r1, r2, r3, r4 = (sb(f"r{k}", [P, SEQS]) for k in range(1, 5))
        weight = sb("weight", [P, SEQS])
        count = sb("count", [P, EXPERTS])
        rowpos = sb("rowpos", [P, SEQS], u32)
        ntiles_i = sb("ntiles_i", [P, EXPERTS], i32)
        ntiles, ends, adjust = (sb(n, [P, EXPERTS]) for n in ("ntiles", "ends", "adjust"))
        tab8 = sb("tab8", [P, EXPERTS, EXPERTS])
        past = sb("past", [P, TILES, EXPERTS])
        past2 = sb("past2", [P, TILES, EXPERTS])
        tile_e, tile_r = sb("tile_e", [P, TILES]), sb("tile_r", [P, TILES])
        tab = sb("tab", [1, 2 * TILES], i32)
        pad_rows = sb("pad_rows", [1, EXPERTS], i32)
        R = 6
        spaces = {"qst": qst[:, :, :, :, :].rearrange("p c h g t -> p (c h g t)").bitcast(fp32), "ctxT": ctxT[:, :]}
        used = {"qst": 0, "ctxT": 0}

        def take(n, place="qst"):
            used[place] += n
            assert used[place] <= spaces[place].shape[-1]
            return spaces[place][:, used[place] - n:used[place]]

        wexp = take(EXPERTS * WROW).rearrange("p (e w) -> p e w", e=EXPERTS)
        w1cur = [take(HID + HC) for u in range(R)]
        rows = [take(RW) for u in range(R)]
        rowsT = [take(P, "ctxT") for u in range(R)]
        hidT = [take(HC * P).rearrange("p (c t) -> p c t", c=HC) for u in range(R)]
        result = [take(D, "ctxT") for u in range(R)]
        tokens = [sb(f"tokens{u}", [P, 1], i32) for u in range(R)]
        b2r = sb("b2r", [P, D])
        b2p = sb("b2p", [P, D], bf16)
        b2m = sb("b2m", [P, D], bf16)
        pick = sb("pick", [P, TILES], bf16)

        bank = [ctx.enter_context(nc.psum_tensor(f"bank{i}", [P, CT], fp32)) for i in range(8)]

        s_w = sem("weights_loaded")
        s_xin = [sem(f"x_{c}_loaded") for c in range(CHUNKS)]
        s_cin = [sem("ctx_chunk_0_loaded"), sem("ctx_others_loaded")]
        s_gates = sem("gates_ready")
        s_zero = sem("stack_zeroed")
        s_ones = sem("ones_ready")
        s_kones = sem("k_ones_loaded")
        s_spare = sem("spare_stored")
        s_rstd = sem("rstd_ready")
        s_veps = sem("variance_plus_eps_ready")
        s_first = sem("first_weights_loaded")
        s_row = sem("row_vectors_loaded")
        s_xb = sem("x_plus_bias_ready")
        s_pool = sem("pool_own_order")
        s_xn = sem("xn_ready")
        s_xt = sem("xn_transposed")
        s_xtc = sem("xnT_ready")
        s_proj = {n: sem(f"{n}_projected") for n in "kq"}
        s_high = {n: sem(f"{n}_high_part_ready") for n in "kq"}
        s_rest = {n: sem(f"{n}_rest_ready") for n in "kq"}
        s_mid = {n: sem(f"{n}_middle_part_ready") for n in "kq"}
        s_part = {n: sem(f"{n}_parts_ready") for n in "kq"}
        s_store = {n: [sem(f"{n}_even_parts_stored"), sem(f"{n}_odd_parts_stored")] for n in "kq"}
        s_v = sem("v_projected")
        s_vc = sem("v_ready")
        s_stack = [sem(f"stack_{c}_loaded") for c in range(CHUNKS)]
        s_chain = sem("dve_own_order")
        s_s1 = sem("score_quarters_ready")
        s_mx = sem("maxima_quarters_taken")
        s_nm = sem("minus_max_ready")
        s_mt = sem("max_transposed")
        s_mtc = sem("max_copied")
        s_mrow = [sem("max_rows_even"), sem("max_rows_odd")]
        s_s2 = sem("shifted_quarters_ready")
        s_exp = sem("probs_quarters_ready")
        s_pv = sem("pv_done")
        s_ot = sem("pv_evacuated")
        s_ott = sem("pv_transposed")
        s_norm = sem("heads_normalised")
        s_ht = sem("heads_transposed")
        s_htc = sem("headsT_ready")
        s_wo = sem("output_projected")
        s_x1 = sem("x1_ready")
        s_rs = sem("sums_inverted")
        s_nh = sem("minus_max_high_ready")
        s_rxn = sem("route_xn_ready")
        s_rxt = sem("route_xn_transposed")
        s_rxtc = sem("route_xnT_ready")
        s_gate = sem("gate_product_ready")
        s_shift = sem("gate_logits_shifted")
        s_gexp = sem("gate_exp_ready")
        s_oh = sem("choice_ready")
        s_rank = sem("ranks_ready")
        s_routed = sem("routed_rows_ready")
        s_scat = sem("routed_rows_scattered")
        s_tab = sem("tile_table_ready")
        s_padrow = sem("pad_rows_ready")
        s_pad = sem("pads_stored")
        s_tile = [sem(f"tile_loaded_{u}") for u in range(R)]
        s_wexp = sem("expert_weights_loaded")
        s_w1 = sem("w1_in_place")
        s_b2 = sem("b2_split")
        s_tt = sem("rows_transposed")
        s_ttc = sem("rowsT_ready")
        s_up = sem("hidden_ready")
        s_ra = sem("relu_by_act")
        s_rv = sem("relu_by_dve")
        s_down = sem("expert_out_ready")
        s_res = sem("result_ready")
        s_out = [sem(f"result_stored_{u}") for u in range(R)]

        class Order:

            def __init__(self, eng, s):
                self.eng, self.sem, self.n, self.base = eng, s, 0, 0

            def after(self, ins):
                self.n += 1
                ins.then_inc(self.sem, 1)
                self.eng.wait_ge(self.sem, self.base + self.n)

            def loop(self, i, length, since):
                self.base, self.n = since + i * length, 0

        def wait(eng, s, value):
            if not (isinstance(value, int) and value <= 0):
                eng.wait_ge(s, value)

        class Item:

            def __init__(self, n, lag, ring, i=None):
                if i is None:
                    self.no = n - lag
                    self.u, self.lap, self.no2 = self.no % ring, self.no // ring, self.no % 2
                else:
                    k = n - lag
                    self.no, self.u, self.lap, self.no2 = ring * i + k, k % ring, i + k // ring, k % 2

        def pipeline(eng, items, first, ring, one_step, more=None):
            def straight(n):
                one_step(lambda lag: Item(n, lag, ring) if 0 <= n - lag < items else None)
            for n in range(first):
                straight(n)
            with eng.Fori(0, (items - first) // ring) as i:
                for k in range(ring):
                    one_step(lambda lag: Item(first + k, lag, ring, i))
            for n in range(items, items + first):
                straight(n)
                if more:
                    more(n - items)

        LAG_MT, LAG_S2, LAG_PV, LAG_OUT = 1, 2, 3, 4
        LAG_UP, LAG_DOWN = 1, 2
        PV_BANKS = (4, 7)
        ROUTE_BANKS = (4, 7)
        QUARTERS = 4
        EXPERTS_FIRST = 11
        assert (TILES - EXPERTS_FIRST) % R == 0 and EXPERTS_FIRST >= LAG_DOWN + R - 1

        def attention(eng, one_step, more=None):
            pipeline(eng, SEQS, LAG_OUT, CHUNK, one_step, more)

        def attention_straight(one_step, more):
            for n in range(SEQS + LAG_OUT):
                one_step(lambda lag: Item(n, lag, CHUNK) if 0 <= n - lag < SEQS else None)
                if n >= SEQS:
                    more(n - SEQS)

        def chunk(c):
            return slice(c * CHUNK, (c + 1) * CHUNK)

        def experts(eng, one_step):
            pipeline(eng, TILES, EXPERTS_FIRST, R, one_step)

        def experts_straight(one_step):
            for n in range(TILES + LAG_DOWN):
                one_step(lambda lag: Item(n, lag, R) if 0 <= n - lag < TILES else None)

        def tok(u):
            return slice(u * QLEN, (u + 1) * QLEN)

        STORES, LOADS = 3, 4

        ALL_W = 16 * 2

        def pads(eng, parity):
            for e in range(parity, EXPERTS, 2):
                first = eng.value_load(pad_rows[0:1, e:e + 1], min_val=0, max_val=EXPERTS * CAP)
                eng.dma_start(rows_dram[ds(first, P), :], spare).then_inc(s_pad, 16)

        block = ctx.enter_context(nc.Block())

        @block.sync
        def _(sp):
            for c in range(CHUNKS):
                sp.dma_start(x[:, chunk(c), :], io["x"][:, chunk(c), :]).then_inc(s_xin[c], 16)
            sp.dma_start(kst[STACK:STACK + 2].rearrange("r c g t -> r (c g t)"), io["ones"]).then_inc(s_kones, 16)
            sp.wait_ge(s_kones, 16)
            def store(c):
                for n in "kq":
                    sp.wait_ge(s_part[n], c + 1)
                    terms = parts_dram[n][c].rearrange("s h d g t -> (h d g) s t")
                    for s0, s1 in ((0, 3), (3, 5), (5, 6)):
                        k = TERM_PARTS[n][s0:s1]
                        src = part[n][c % 2][:, k[0]:k[0] + len(set(k)), :]
                        if len(set(k)) < len(k):
                            src = src.to_broadcast([P, len(k), CT])
                        sp.dma_start(terms[:, s0:s1, :], src).then_inc(s_store[n][c % 2], 16)

            def load(c):
                for n in "kq":
                    sp.wait_ge(s_store[n][c % 2], 16 * STORES * (c // 2 + 1))
                    if n == "q":
                        sp.wait_ge(s_zero, c + 1)
                    for hp in range(2):
                        dst = kst[hp * TERMS * HD:(hp + 1) * TERMS * HD, c] if n == "k" else \
                            qst[hp * TERMS * HD:(hp + 1) * TERMS * HD, c, hp]
                        sp.dma_start(dst.rearrange("r g t -> r (g t)"),
                                     parts_dram[n][c, :, hp].rearrange("s d g t -> s d (g t)")).then_inc(s_stack[c], 16)

            store(0)
            store(1)
            load(0)
            sp.wait_ge(s_mrow[0], 16)
            load(1)
            store(2)
            sp.wait_ge(s_mrow[1], 16)
            load(2)
            store(3)
            sp.wait_ge(s_mrow[0], 2 * 16)
            load(3)

            sp.wait_ge(s_s1, QUARTERS * SEQS)
            sp.wait_ge(s_s2, QUARTERS * SEQS)
            for e in range(EXPERTS):
                sp.dma_start(wexp[:, e, :], io["wexp"][e * P:(e + 1) * P, :]).then_inc(s_wexp, 16)
            sp.wait_ge(s_padrow, 1)
            pads(sp, 0)
            sp.wait_ge(s_pad, 16 * EXPERTS)
            sp.wait_ge(s_spare, 16)
            sp.wait_ge(s_scat, 16 * SEQS)

            sp.wait_ge(s_tab, 1)
            def load_tile(item):
                if t := item(0):
                    first = sp.value_load(tab[0:1, ds(t.no + TILES, 1)], min_val=0, max_val=EXPERTS * CAP)
                    wait(sp, s_res, t.no - R + 1)
                    sp.dma_start(rows[t.u], rows_dram[ds(first, P), :]).then_inc(s_tile[t.u], 16)
            experts(sp, load_tile)

        @block.gpsimd
        def _(pool):
            order = Order(pool, s_pool)
            G = nc.gpsimd
            order.after(G.memset(power[:, :], -0.5))
            for c in range(CHUNKS + 1):
                if c < CHUNKS:
                    pool.wait_ge(s_veps, c + 1)
                    G.tensor_tensor(rstd[:, chunk(c)], veps[:, chunk(c)], power[:, chunk(c)], ALU.pow).then_inc(s_rstd, 1)
                if c:
                    G.memset(qst[0:STACK, c - 1].rearrange("r h g t -> r (h g t)").bitcast(u32), 0).then_inc(s_zero, 1)
            pool.wait_ge(s_gates, 1)
            for c in range(CHUNKS):
                pool.wait_ge(s_xin[c], 16)
            pool.wait_ge(s_xn, CHUNKS)
            order.after(G.tensor_tensor(bo, bo, gates[:, 0:1].to_broadcast([P, D]), ALU.mult))
            G.tensor_tensor(x[:, :, :], x[:, :, :], bo.unsqueeze(1).to_broadcast([P, SEQS, D]), ALU.add).then_inc(s_xb, 1)
            pool.wait_ge(s_w, ALL_W)
            pool.dma_start(rows_dram[EXPERTS * CAP:EXPERTS * CAP + P, :], spare).then_inc(s_spare, 16)
            for c in range(CHUNKS):
                pool.wait_ge(s_veps, CHUNKS + c + 1)
                G.tensor_tensor(rstd[:, chunk(c)], veps[:, chunk(c)], power[:, chunk(c)], ALU.pow).then_inc(s_rstd, 1)
            for c in range(CHUNKS):
                pool.wait_ge(s_routed, c + 1)
                for t in range(c * CHUNK, (c + 1) * CHUNK):
                    pool.indirect_dma_start(rows_dram, bass.IndirectOffsetOnAxis(ap=rowpos[:, t:t + 1], axis=0),
                                            routed[:, t, :], None).then_inc(s_scat, 16)
            for t in range(TILES):
                pool.wait_ge(s_res, t + 1)
                pool.indirect_dma_start(io["out"], bass.IndirectOffsetOnAxis(
                    ap=tokens[t % R][:, :].bitcast(u32), axis=0), result[t % R], None,
                    bounds_check=TOKENS - 1, oob_is_err=False).then_inc(s_out[t % R], 16)
            for u in range(R):
                pool.wait_ge(s_out[u], 16 * len(range(u, TILES, R)))

        @block.scalar
        def _(act):
            act.dma_start(packs["first"][:, :], io["first"]).then_inc(s_first, 16)
            act.dma_start(ctxT[:, 0:CT], io["ctxT"][:, 0:CT]).then_inc(s_cin[0], 16)
            act.dma_start(packs["row"][:, :], io["row"].to_broadcast([P, packs["row"].shape[1]])).then_inc(s_row, 16)
            act.dma_start(ctxT[:, CT:TOKENS], io["ctxT"][:, CT:TOKENS]).then_inc(s_cin[1], 16)
            act.dma_start(packs["half"][:, :], io["half"]).then_inc(s_w, 16)
            act.dma_start(packs["late"][:, :], io["late"]).then_inc(s_w, 16)
            act.wait_ge(s_row, 16)
            nc.scalar.activation(gates[:, :], gate_in, ACT.Tanh).then_inc(s_gates, 1)
            act.wait_ge(s_first, 16)
            for c in range(CHUNKS):
                act.wait_ge(s_xt, c + 1)
                wait(act, s_proj["q"], c)
                nc.scalar.activation(xnT[:, :], bank[0][:, :], ACT.Copy).then_inc(s_xtc, 1)
                for n, b_, bias in (("k", 1, bk), ("q", 2, bq)):
                    act.wait_ge(s_proj[n], c + 1)
                    wait(act, s_store[n][c % 2], 16 * STORES * (c // 2))
                    nc.scalar.activation(part[n][c % 2][:, 0, :], bank[b_][:, :], ACT.Identity, bias=bias).then_inc(s_high[n], 1)
                if c == 0:
                    act.wait_ge(s_ones, 1)
                act.wait_ge(s_v, c + 1)
                nc.scalar.activation(vall[:, chunk(c), :, 0:HD], bank[4 + c][:, :].rearrange("p (b h d) -> p b h d", b=CHUNK, h=HEADS),
                                     ACT.Copy).then_inc(s_vc, 1)
                for n in "kq":
                    act.wait_ge(s_rest[n], c + 1)
                    nc.scalar.activation(part[n][c % 2][:, 1, :], rest[n][:, :], ACT.Copy).then_inc(s_mid[n], 1)
            act.wait_ge(s_vc, CHUNKS)
            act.wait_ge(s_w, ALL_W)
            for b_ in PV_BANKS:
                nc.scalar.activation(bank[b_][:, :].rearrange("p (k d) -> p k d", k=QUARTERS),
                                     spare[:, 0:P].unsqueeze(1).to_broadcast([P, QUARTERS, P]), ACT.Copy).then_inc(s_vc, 1)

            def one_step(item):
                m, s, o = item(LAG_MT), item(LAG_S2), item(LAG_OUT)
                for t in range(QUARTERS):
                    if t == 0 and o:
                        act.wait_ge(s_pv, o.no + 1)
                        nc.scalar.activation(oT[o.no2][:, :], bank[PV_BANKS[o.no2]][:, :], ACT.Copy).then_inc(s_ot, 1)
                    if t == 1 and m:
                        act.wait_ge(s_mt, m.no + 1)
                        wait(act, s_mrow[m.no2], 16 * (m.no // 2 if isinstance(m.no, int) else 2 * m.lap + m.u // 2))
                        nc.scalar.activation(nmaxT[m.no2][:, :], bank[6][0:2 * HEADS, 0:P // 2].bitcast(bf16), ACT.Copy)\
                          .then_inc(s_mtc, 1)
                    if t == 3 and o:
                        act.wait_ge(s_ht, o.no + 1)
                        wait(act, s_wo, o.no)
                        nc.scalar.activation(headsT[:, :], bank[6][:, 128:256], ACT.Copy).then_inc(s_htc, 1)
                    if s:
                        if t == 0:
                            wait(act, s_pv, s.no - 1)
                        act.wait_ge(s_s2, QUARTERS * s.no + t + 1)
                        nc.scalar.activation(probs[s.no2][:, 4 * t:4 * t + 4, :].rearrange("p h q -> p (h q)"),
                                             bank[2 + t % 2][:, :], ACT.Exp, scale=HD ** -0.5).then_inc(s_exp, 1)
                    if t == 1 and m:
                        act.wait_ge(s_mtc, m.no + 1)
                        act.dma_start(qst[STACK:STACK + 2, ds(m.lap, 1), :, :, tok(m.u)].rearrange("s c h g t -> s (c h g) t"),
                                      nmaxT[m.no2][:, :]).then_inc(s_mrow[m.no2], 16)

            def turned(c):
                act.wait_ge(s_rxt, c + 1)
                nc.scalar.activation(ctxT[:, c * CT:(c + 1) * CT], bank[c][:, :], ACT.Copy).then_inc(s_rxtc, 1)

            def more(n):
                if n == 2:
                    turned(0)
            attention(act, one_step, more)

            def gate_exp(h):
                half = slice(h * HALF, (h + 1) * HALF)
                act.wait_ge(s_shift, h + 1)
                nc.scalar.activation(escore[:, half, :], logit[:, half, :], ACT.Exp).then_inc(s_gexp, 1)

            for c in range(1, CHUNKS):
                turned(c)
            gate_exp(0)
            gate_exp(1)

            act.wait_ge(s_padrow, 1)
            pads(act, 1)

            def expert_step(item):
                if t := item(0):
                    act.wait_ge(s_tt, t.no + 1)
                    wait(act, s_up, t.no - R + 1)
                    nc.scalar.activation(rowsT[t.u], bank[0][:, 0:P], ACT.Copy).then_inc(s_ttc, 1)
                if k := item(LAG_UP):
                    act.wait_ge(s_up, k.no + 1)
                    wait(act, s_down, k.no - R + 1)
                    for c in range(2):
                        ins = nc.scalar.activation(hidT[k.u][:, c, :], bank[1 + k.no2][:, c * P:(c + 1) * P], ACT.Relu,
                                                   bias=w1cur[k.u][:, HID + c:HID + c + 1])
                    ins.then_inc(s_ra, 1)
            experts(act, expert_step)

        @block.vector
        def _(dve):
            order = Order(dve, s_chain)
            V = nc.vector
            V.memset(onesb[:, :], 1.0)
            V.memset(vall[:, :, :, HD:VW], 1.0)
            V.memset(chosenb[:, SEQS, :], 0.0).then_inc(s_ones, 1)
            dve.wait_ge(s_first, 16)
            def ln_stats(c, src):
                for b in range(c * CHUNK, (c + 1) * CHUNK):
                    ins = V.bn_stats(stats[:, b, :], src[:, b, :])
                order.after(ins)
                for b in range(c * CHUNK, (c + 1) * CHUNK):
                    ins = V.bn_aggr(mv[:, b, :], stats[:, b, :])
                order.after(ins)
                V.tensor_scalar(veps[:, chunk(c)], mv[:, chunk(c), 1], EPS, None, ALU.add).then_inc(s_veps, 1)

            def ln_rows(c, src, so_far, done):
                dve.wait_ge(s_rstd, so_far + c + 1)
                for b in range(c * CHUNK, (c + 1) * CHUNK):
                    ins = V.tensor_scalar(xn[:, b, :], src[:, b, :], mv[:, b, 0:1], rstd[:, b:b + 1], ALU.subtract, ALU.mult)
                ins.then_inc(done, 1)

            def take_rest(n, c, b_, bias):
                dve.wait_ge(s_high[n], c + 1)
                wait(dve, s_part[n], c)
                V.scalar_tensor_tensor(out=rest[n][:, :], in0=bank[b_][:, :], scalar=bias, in1=part[n][c % 2][:, 0, :],
                                       op0=ALU.add, op1=ALU.subtract).then_inc(s_rest[n], 1)

            def low_part(n, c):
                dve.wait_ge(s_mid[n], c + 1)
                V.tensor_tensor(part[n][c % 2][:, 2, :], rest[n][:, :], part[n][c % 2][:, 1, :],
                                ALU.subtract).then_inc(s_part[n], 1)

            for c in range(-2, CHUNKS):
                if c + 2 < CHUNKS:
                    dve.wait_ge(s_xin[c + 2], 16)
                    ln_stats(c + 2, x)
                if c >= 0:
                    take_rest("k", c, 1, bk)
                    take_rest("q", c, 2, bq)
                if c + 2 < CHUNKS:
                    ln_rows(c + 2, x, 0, s_xn)
                if c >= 0:
                    low_part("k", c)
                    low_part("q", c)
            dve.wait_ge(s_w, ALL_W)
            V.tensor_copy(routed[:, :, 2 * D:RW].bitcast(i32).rearrange("p t o -> p (t o)"), token_no)
            dve.wait_ge(s_gates, 1)

            def one_step(item):
                m, o = item(0), item(LAG_OUT)
                if m and isinstance(m.no, int) and m.no == LAG_OUT - 1:
                    dve.wait_ge(s_xb, 1)
                for t in range(QUARTERS):
                    if t == 2 and o:
                        dve.wait_ge(s_ott, o.no + 1)
                        wide = bank[5][:, :].rearrange("p (h w) -> p h w", w=32)
                        V.reciprocal(rsum[:, :], wide[:, :, HD]).then_inc(s_rs, 1)
                        dve.wait_ge(s_rs, o.no + 1)
                        wait(dve, s_ht, o.no)
                        V.tensor_tensor(heads_out[:, :, :], wide[:, :, 0:HD],
                                        rsum[:, :].unsqueeze(2).to_broadcast([P, HEADS, HD]), ALU.mult).then_inc(s_norm, 1)
                    if m:
                        dve.wait_ge(s_s1, QUARTERS * m.no + t + 1)
                        V.reduce_max(smax[m.no2][:, :].rearrange("p (h g) -> p g h", h=2)[:, 2 * t:2 * t + 2, :],
                                     bank[t % 2][:, :].rearrange("p (g h k) -> p g h k", g=2, h=2), axis=AX.X).then_inc(s_mx, 1)
                if m:
                    wait(dve, s_mt, m.no - 1)
                    dve.wait_ge(s_mx, QUARTERS * (m.no + 1))
                    V.tensor_scalar(nmax[m.no2][:, 0, :], smax[m.no2][:, :], -1.0, None, ALU.mult).then_inc(s_nh, 1)
                if o:
                    dve.wait_ge(s_wo, o.no + 1)
                    row = ds(o.no, 1)
                    V.scalar_tensor_tensor(out=x1[:, row, :].rearrange("p a d -> p (a d)"), in0=bank[6][:, 256:256 + D],
                                           scalar=gates[:, 0:1], in1=x[:, row, :].rearrange("p a d -> p (a d)"),
                                           op0=ALU.mult, op1=ALU.add).then_inc(s_x1, 1)
                if m:
                    dve.wait_ge(s_nh, m.no + 1)
                    V.scalar_tensor_tensor(out=nmax[m.no2][:, 1, :], in0=smax[m.no2][:, :], scalar=-1.0,
                                           in1=nmax[m.no2][:, 0, :], op0=ALU.mult, op1=ALU.subtract).then_inc(s_nm, 1)

            def more(n):
                if n < CHUNKS - 1:
                    dve.wait_ge(s_x1, CHUNK * (n + 1))
                    ln_stats(n, x1)
                if n >= 1:
                    ln_rows(n - 1, x1, CHUNKS, s_rxn)

            E8 = [P, HALF, EXPERTS]

            def halves(h):
                half = slice(h * HALF, (h + 1) * HALF)
                return [a[:, half, :] for a in (logit, escore, score, score2, hit, chosen)], [a[:, half] for a in (r1, r2, r3, r4)]

            def wide(a):
                return a.unsqueeze(2).to_broadcast(E8)

            def all_rows(a):
                return a.unsqueeze(1).to_broadcast(E8)

            def shift_logits(h):
                (logit_, *_), (r1_, *_) = halves(h)
                dve.wait_ge(s_gate, h + 1)
                order.after(V.tensor_tensor(logit_, bank[ROUTE_BANKS[h]][:, 0:HALF * EXPERTS].rearrange(
                    "p (t e) -> p t e", t=HALF), all_rows(gate_b), ALU.add))
                order.after(V.reduce_max(r1_, logit_, axis=AX.X))
                V.tensor_tensor(logit_, logit_, wide(r1_), ALU.subtract).then_inc(s_shift, 1)

            def best(h):
                (_, escore_, score_, _, hit_, _), (r1_, r2_, _, _) = halves(h)
                dve.wait_ge(s_gexp, h + 1)
                order.after(V.reduce_sum(r1_, escore_, axis=AX.X))
                order.after(V.reciprocal(r2_, r1_))
                order.after(V.tensor_tensor(score_, escore_, wide(r2_), ALU.mult))
                order.after(V.reduce_max(r1_, score_, axis=AX.X))
                order.after(V.tensor_tensor(hit_, score_, wide(r1_), ALU.is_equal))
                order.after(V.tensor_tensor(hit_, hit_, all_rows(eights), ALU.mult))
                order.after(V.reduce_max(r2_, hit_, axis=AX.X))
                order.after(V.tensor_tensor(hit_, all_rows(eights), wide(r2_), ALU.is_equal))

            def choose(h):
                (_, _, score_, score2_, hit_, chosen_), (r1_, r2_, r3_, r4_) = halves(h)
                half = slice(h * HALF, (h + 1) * HALF)
                order.after(V.scalar_tensor_tensor(out=score2_, in0=hit_, scalar=-2.0, in1=score_, op0=ALU.mult, op1=ALU.add))
                order.after(V.reduce_max(r3_, score2_, axis=AX.X))
                order.after(V.tensor_tensor(hit_, score2_, wide(r3_), ALU.is_equal))
                order.after(V.tensor_tensor(hit_, hit_, all_rows(eights), ALU.mult))
                order.after(V.reduce_max(r4_, hit_, axis=AX.X))
                order.after(V.tensor_tensor(r4_, r4_, r2_, ALU.subtract))
                order.after(V.tensor_scalar(r4_, r4_, 0.0, None, ALU.min))
                order.after(V.scalar_tensor_tensor(out=r4_, in0=r3_, scalar=0.0, in1=r4_, op0=ALU.is_gt, op1=ALU.mult))
                order.after(V.tensor_tensor(r2_, r2_, r4_, ALU.add))
                order.after(V.tensor_tensor(chosen_, all_rows(eights), wide(r2_), ALU.is_equal))
                V.tensor_copy(chosenb[:, half, :], chosen_).then_inc(s_oh, 1)
                order.after(V.tensor_tensor(hit_, chosen_, score_, ALU.mult))
                order.after(V.reduce_sum(weight[:, half], hit_, axis=AX.X))
                weigh(2 * h)
                dve.wait_ge(s_rank, h + 1)
                ranks = bank[ROUTE_BANKS[h]][:, 256:256 + (HALF + 1) * EXPERTS].rearrange("p (t e) -> p t e", e=EXPERTS)
                order.after(V.tensor_tensor(hit_, ranks[:, 0:HALF, :], all_rows(region), ALU.add))
                if h == 1:
                    V.tensor_tensor(pad_rows[:, :], region[0:1, :], ranks[0:1, HALF, :], ALU.add).then_inc(s_padrow, 1)
                    V.tensor_copy(count[:, :], ranks[:, HALF, :])
                order.after(V.tensor_tensor(hit_, hit_, chosen_, ALU.mult))
                order.after(V.reduce_sum(r1_, hit_, axis=AX.X))
                V.tensor_copy(rowpos[:, half], r1_).then_inc(s_routed, 1)
                weigh(2 * h + 1).then_inc(s_routed, 1)

            def weigh(c):
                dve.wait_ge(s_rxt, c + 1)
                return V.tensor_tensor(xn[:, chunk(c), :], xn[:, chunk(c), :],
                                       weight[:, chunk(c)].unsqueeze(2).to_broadcast([P, CHUNK, D]), ALU.mult)

            attention(dve, one_step, more)

            dve.wait_ge(s_x1, SEQS)
            ln_stats(CHUNKS - 1, x1)
            ln_rows(CHUNKS - 1, x1, CHUNKS, s_rxn)
            shift_logits(0)
            best(0)
            choose(0)
            parts3 = [slice(32 * k, 32 * k + EXPERTS) for k in range(NPART)]
            order.after(V.tensor_copy(b2p[:, :], b2f))
            order.after(V.tensor_tensor(b2r[:, :], b2f, b2p[:, :], ALU.subtract))
            order.after(V.tensor_copy(b2m[:, :], b2r[:, :]))
            V.tensor_copy(b2p[parts3[1], :], b2m[parts3[1], :])
            V.tensor_tensor(b2p[parts3[2], :], b2r[parts3[2], :], b2m[parts3[2], :], ALU.subtract).then_inc(s_b2, 1)
            shift_logits(1)
            best(1)
            choose(1)
            dve.wait_ge(s_routed, CHUNKS)
            order.after(V.tensor_scalar(ntiles_i[:, :], count[:, :], float(P - 1), None, ALU.add))
            order.after(V.tensor_scalar(ntiles_i[:, :], ntiles_i[:, :], 7, None, ALU.arith_shift_right))
            order.after(V.tensor_copy(ntiles[:, :], ntiles_i[:, :]))
            E88 = [P, EXPERTS, EXPERTS]
            order.after(V.tensor_tensor(tab8[:, :, :], upto, ntiles[:, :].unsqueeze(1).to_broadcast(E88), ALU.mult))
            order.after(V.reduce_sum(ends[:, :], tab8[:, :, :], axis=AX.X))
            ET = [P, TILES, EXPERTS]
            order.after(V.tensor_scalar(adjust[:, :], ntiles[:, :], -float(P), float(CAP), ALU.mult, ALU.add))
            order.after(V.tensor_tensor(past[:, :, :], ends[:, :].unsqueeze(1).to_broadcast(ET),
                                        tiles_no.unsqueeze(2).to_broadcast(ET), ALU.is_le))
            order.after(V.reduce_sum(tile_e[:, :], past[:, :, :], axis=AX.X))
            order.after(V.tensor_tensor(past2[:, :, :], past[:, :, :], adjust[:, :].unsqueeze(1).to_broadcast(ET), ALU.mult))
            order.after(V.reduce_sum(tile_r[:, :], past2[:, :, :], axis=AX.X))
            order.after(V.scalar_tensor_tensor(out=tile_r[:, :], in0=tiles_no[:, :], scalar=float(P), in1=tile_r[:, :],
                                               op0=ALU.mult, op1=ALU.add))
            order.after(V.tensor_scalar(tile_e[:, :], tile_e[:, :], float(EXPERTS - 1), None, ALU.min))
            V.tensor_scalar(pick[:, :], tile_e[:, :], my_expert, None, ALU.is_equal)
            V.tensor_scalar(tab[:, 0:TILES], tile_e[0:1, :], float(EXPERTS - 1), None, ALU.min)
            V.tensor_scalar(tab[:, TILES:2 * TILES], tile_r[0:1, :], float(EXPERTS * CAP), None, ALU.min).then_inc(s_tab, 1)

            dve.wait_ge(s_wexp, 16 * EXPERTS)
            dve.wait_ge(s_tab, 1)

            def expert_step(item):
                if t := item(0):
                    e = dve.value_load(tab[0:1, ds(t.no, 1)], min_val=0, max_val=EXPERTS - 1)
                    wait(dve, s_down, t.no - R + 1)
                    wait(dve, s_rv, t.no - R + 1)
                    V.tensor_copy(w1cur[t.u], wexp[:, ds(e, 1), HC * D:WROW].rearrange("p a w -> p (a w)")).then_inc(s_w1, 1)
                if k := item(LAG_UP):
                    dve.wait_ge(s_up, k.no + 1)
                    dve.wait_ge(s_w1, k.no + 1)
                    for c in range(2, HC):
                        ins = V.tensor_scalar(hidT[k.u][:, c, :], bank[3 + k.no2][:, (c - 2) * P:(c - 1) * P],
                                              w1cur[k.u][:, HID + c:HID + c + 1], 0.0, ALU.add, ALU.max)
                    ins.then_inc(s_rv, 1)
                if d := item(LAG_DOWN):
                    dve.wait_ge(s_down, d.no + 1)
                    wait(dve, s_out[d.u], 16 * d.lap)
                    V.tensor_copy(tokens[d.u][:, :], rows[d.u][:, 2 * D:RW].bitcast(i32))
                    V.scalar_tensor_tensor(out=result[d.u], in0=bank[5 + d.no2][:, 0:D], scalar=gates[:, 1:2],
                                           in1=rows[d.u][:, 0:D], op0=ALU.mult, op1=ALU.add).then_inc(s_res, 1)
            experts(dve, expert_step)

        @block.tensor
        def _(pe):
            M = nc.tensor.matmul

            def at(view):
                return view.rearrange("r c t -> r (c t)")

            pe.wait_ge(s_first, 16)
            for c in range(CHUNKS):
                wait(pe, s_rest["k"], c)
                if c < 2:
                    pe.wait_ge(s_cin[c], 16)
                M(bank[1][:, :], wk, ctxT[:, c * CT:(c + 1) * CT], start=True, stop=True).then_inc(s_proj["k"], 1)
                pe.wait_ge(s_xn, c + 1)
                for t in range(CHUNK):
                    ins = nc.tensor.transpose(bank[0][:, t * P:(t + 1) * P], xn[:, c * CHUNK + t, :], ident)
                ins.then_inc(s_xt, 1)
                def values():
                    if c == 0:
                        pe.wait_ge(s_row, 16)
                    for b in range(c * CHUNK, (c + 1) * CHUNK):
                        out = bank[4 + c][:, (b % CHUNK) * D:(b % CHUNK + 1) * D]
                        M(out, ctxT[:, b * QLEN:(b + 1) * QLEN], wv, start=True, stop=False)
                        ins = M(out, one_row[0:1, :], bv[0:1, :], start=False, stop=True)
                    ins.then_inc(s_v, 1)

                if c:
                    values()
                pe.wait_ge(s_xtc, c + 1)
                wait(pe, s_rest["q"], c)
                M(bank[2][:, :], wq, xnT[:, :], start=True, stop=True).then_inc(s_proj["q"], 1)
                if not c:
                    values()
            pe.wait_ge(s_rest["q"], CHUNKS)
            pe.wait_ge(s_ones, 1)
            pe.wait_ge(s_vc, CHUNKS)

            def one_step(item):
                q, m, s, v, o = (item(lag) for lag in (0, LAG_MT, LAG_S2, LAG_PV, LAG_OUT))
                for t in range(QUARTERS):
                    if q:
                        if t == 0 and q.u == 0:
                            pe.wait_ge(s_stack[q.lap], 16 * LOADS)
                        wait(pe, s_mx, QUARTERS * q.no + t - 1)
                        for k in range(4):
                            g, hp = 2 * t + k // 2, k % 2
                            ins = M(bank[t % 2][:, k * P:(k + 1) * P], at(qst[0:STACK, ds(q.lap, 1), hp, g, tok(q.u)]),
                                    at(kst[0:STACK, ds(q.lap, 1), g, tok(q.u)]), start=True, stop=True)
                        ins.then_inc(s_s1, 1)
                    if s:
                        if t == 0:
                            pe.wait_ge(s_mrow[s.no2], 16 * ((s.no // 2 if isinstance(s.no, int) else 2 * s.lap + s.u // 2) + 1))
                        wait(pe, s_exp, QUARTERS * s.no + t - 1)
                        for k in range(2):
                            g = 2 * t + k
                            ins = M(bank[2 + t % 2][:, 256 * k:256 * (k + 1)], at(kst[:, ds(s.lap, 1), g, tok(s.u)]),
                                    qst[0:STACK + 2, ds(s.lap, 1), :, g, tok(s.u)].rearrange("r c h t -> r (c h) t"),
                                    start=True, stop=True)
                        ins.then_inc(s_s2, 1)
                    if v:
                        if t == 0:
                            if v.no == 0:
                                pe.wait_ge(s_vc, CHUNKS + 2)
                            wait(pe, s_ot, v.no - 1)
                        pe.wait_ge(s_exp, QUARTERS * v.no + t + 1)
                        for j in range(4):
                            ins = M(bank[PV_BANKS[v.no2]][32 * j:32 * j + VW, t * P:(t + 1) * P],
                                    vall[:, v.no, 4 * t + j, :], probs[v.no2][:, 4 * t + j, :], start=True, stop=True)
                        if t == QUARTERS - 1:
                            ins.then_inc(s_pv, 1)
                    if t == 0 and m:
                        pe.wait_ge(s_nm, m.no + 1)
                        wait(pe, s_x1, m.no - (LAG_OUT - LAG_MT))
                        wait(pe, s_mtc, m.no)
                        nc.tensor.transpose(bank[6][0:2 * HEADS, 0:P // 2].bitcast(bf16),
                                            nmax[m.no2][:, :, :].rearrange("p s h -> p (s h)"), identb).then_inc(s_mt, 1)
                    if t == 1 and o:
                        pe.wait_ge(s_ot, o.no + 1)
                        wait(pe, s_norm, o.no)
                        for k in range(QUARTERS):
                            ins = nc.tensor.transpose(bank[5][:, k * P:(k + 1) * P], oT[o.no2][:, k * P:(k + 1) * P], ident)
                        ins.then_inc(s_ott, 1)
                    if t == 2 and o:
                        pe.wait_ge(s_norm, o.no + 1)
                        pe.wait_ge(s_mtc, min(o.no + LAG_OUT, SEQS))
                        nc.tensor.transpose(bank[6][:, 128:256], heads_out[:, :, :].rearrange("p h d -> p (h d)"),
                                            ident).then_inc(s_ht, 1)
                    if t == 3 and o:
                        pe.wait_ge(s_htc, o.no + 1)
                        M(bank[6][:, 256:256 + D], headsT[:, :], wo, start=True, stop=True).then_inc(s_wo, 1)

            def turn(c):
                pe.wait_ge(s_rxn, c + 1)
                for t in range(CHUNK):
                    ins = nc.tensor.transpose(bank[c][:, t * P:(t + 1) * P], xn[:, c * CHUNK + t, :], ident)
                ins.then_inc(s_rxt, 1)

            def gate(h):
                pe.wait_ge(s_ot, SEQS - 1 + h)
                for b in range(h * HALF, (h + 1) * HALF):
                    if b % CHUNK == 0:
                        pe.wait_ge(s_rxtc, b // CHUNK + 1)
                    k = b - h * HALF
                    ins = M(bank[ROUTE_BANKS[h]][:, k * EXPERTS:(k + 1) * EXPERTS], ctxT[:, b * P:(b + 1) * P], gate_w,
                            start=True, stop=True)
                ins.then_inc(s_gate, 1)

            def rank(h):
                pe.wait_ge(s_oh, h + 1)
                width = HALF + h
                ranks = bank[ROUTE_BANKS[h]][:, 256:256 + width * EXPERTS].rearrange("p (t e) -> p t e", e=EXPERTS)
                earlier = SEQS if h else HALF - 1
                M(ranks, before, chosenb[:, h * HALF:h * HALF + width, :], start=True, stop=False)
                for b in range(earlier):
                    k = max(b + 1 - h * HALF, 0)
                    ins = M(ranks[:, k:, :], onesb[:, :], chosenb[:, b:b + 1, :].to_broadcast([P, width - k, EXPERTS]),
                            start=False, stop=b == earlier - 1)
                ins.then_inc(s_rank, 1)

            def more(n):
                if n == 2:
                    turn(0)
            attention_straight(one_step, more)

            turn(1)
            gate(0)
            turn(2)
            turn(3)
            rank(0)
            gate(1)
            rank(1)

            pe.wait_ge(s_tab, 1)
            pe.wait_ge(s_wexp, 16 * EXPERTS)
            pe.wait_ge(s_b2, 1)

            def expert_step(item):
                if t := item(0):
                    pe.wait_ge(s_tile[t.u], 16 * (t.lap + 1))
                    wait(pe, s_ttc, t.no)
                    nc.tensor.transpose(bank[0][:, 0:P], rows[t.u][:, D:2 * D], ident).then_inc(s_tt, 1)
                if k := item(LAG_UP):
                    pe.wait_ge(s_ttc, k.no + 1)
                    pe.wait_ge(s_w1, k.no + 1)
                    wait(pe, s_ra, k.no - 1)
                    wait(pe, s_rv, k.no - 1)
                    for c in range(HC):
                        out = bank[(1 if c < 2 else 3) + k.no2][:, c % 2 * P:(c % 2 + 1) * P]
                        ins = M(out, w1cur[k.u][:, c * P:(c + 1) * P], rowsT[k.u], start=True, stop=True)
                    ins.then_inc(s_up, 1)
                if d := item(LAG_DOWN):
                    e = pe.value_load(tab[0:1, ds(d.no, 1)], min_val=0, max_val=EXPERTS - 1)
                    wait(pe, s_res, d.no - 1)
                    out = bank[5 + d.no2][:, 0:D]
                    M(out, pick[:, ds(d.no, 1)].to_broadcast([P, P]), b2p[:, :], start=True, stop=False)
                    pe.wait_ge(s_ra, d.no + 1)
                    pe.wait_ge(s_rv, d.no + 1)
                    for c in range(HC):
                        ins = M(out, hidT[d.u][:, c, :], wexp[:, ds(e, 1), c * D:(c + 1) * D].rearrange("p a d -> p (a d)"),
                                start=False, stop=c == HC - 1)
                    ins.then_inc(s_down, 1)
            experts_straight(expert_step)


def kernel(x, ctx_1024, g_xattn, g_ffn, L0_xattn_Wq, L0_xattn_bq, L0_xattn_Wk, L0_xattn_bk, L0_xattn_Wv, L0_xattn_bv,
           L0_xattn_Wo, L0_xattn_bo, L0_ffn_gate_w, L0_ffn_gate_b, L0_ffn_w1, L0_ffn_b1, L0_ffn_w2, L0_ffn_b2):
    import concourse.bacc as bacc
    from concourse.bass_utils import run_bass_kernel_spmd
    import ml_dtypes

    a = {k: np.asarray(v) for k, v in dict(
        x=x, ctx=ctx_1024, wq=L0_xattn_Wq, bq=L0_xattn_bq, wk=L0_xattn_Wk, bk=L0_xattn_bk, wv=L0_xattn_Wv,
        bv=L0_xattn_bv, wo=L0_xattn_Wo, bo=L0_xattn_bo, gw=L0_ffn_gate_w, gb=L0_ffn_gate_b, w1=L0_ffn_w1,
        b1=L0_ffn_b1, w2=L0_ffn_w2, b2=L0_ffn_b2, gx=g_xattn, gf=g_ffn).items()}

    def by_parity(w):
        return w.reshape(PAIRS, 2, HD, -1).transpose(1, 2, 0, 3).reshape(D, -1)

    f, e = np.float32, np.arange(EXPERTS)
    spare = np.zeros((P, RW), f)
    spare[:, 2 * D] = np.full(P, TOKENS, np.int32).view(f)
    b2f, mine = np.zeros((P, D), f), np.full((P, 1), -1, f)
    for k in range(NPART):
        b2f[32 * k:32 * k + EXPERTS], mine[32 * k:32 * k + EXPERTS, 0] = a["b2"], e
    values = {
        "wq": by_parity(a["wq"]).T, "wk": by_parity(a["wk"]).T, "wv": a["wv"].T, "wo": a["wo"].T,
        "bq": by_parity(a["bq"]), "bk": by_parity(a["bk"]), "bv": a["bv"][None], "one_row": np.ones((1, P), f), "bo": a["bo"][None],
        "gates": np.concatenate([a["gx"], a["gf"]])[None], "gate_w": a["gw"], "gate_b": a["gb"][None],
        "b2f": b2f, "my_expert": mine, "ident": np.eye(P, dtype=f), "identb": np.eye(P, dtype=ml_dtypes.bfloat16),
        "before": np.triu(np.ones((P, P)), 1).astype(ml_dtypes.bfloat16),
        "eights": np.tile((EXPERTS - e).astype(f), (P, 1)), "region": np.tile((e * CAP).astype(f), (P, 1)),
        "upto": np.tile((e[None, :] <= e[:, None]).astype(f).reshape(1, -1), (P, 1)),
        "tiles_no": np.tile(np.arange(TILES, dtype=f), (P, 1)),
        "token_no": (np.arange(SEQS)[None, :] * P + np.arange(P)[:, None]).astype(np.int32).view(f),
        "spare": spare,
    }
    arrays = {
        **{n: np.concatenate([values[k] for k, _ in fields], axis=1)
           for n, fields in (("first", FIRST_PACK), ("late", LATE_PACK), ("half", HALF_PACK), ("row", ROW_PACK))},
        "ones": np.ones((2, PAIRS * TOKENS), ml_dtypes.bfloat16),
        "x": a["x"].transpose(1, 0, 2), "ctxT": a["ctx"].transpose(2, 0, 1).reshape(D, TOKENS),
        "wexp": np.concatenate([a["w2"].reshape(EXPERTS, HC, P, D).transpose(0, 2, 1, 3).reshape(EXPERTS, P, HC * D), a["w1"],
                                a["b1"].reshape(EXPERTS, HC, P).transpose(0, 2, 1)], axis=2).reshape(EXPERTS * P, WROW),
    }
    nc = bacc.Bacc("TRN2", target_bir_lowering=False, num_devices=1)
    io, feed = {}, {}
    for name, v in arrays.items():
        v = np.ascontiguousarray(v)
        feed[f"in_{name}"] = v
        io[name] = nc.dram_tensor(f"in_{name}", v.shape, mybir.dt.from_np(v.dtype), kind="ExternalInput").ap()
    io["out"] = nc.dram_tensor("out", [TOKENS, D], mybir.dt.float32, kind="ExternalOutput").ap()
    build(nc, io)
    r = run_bass_kernel_spmd(nc, [feed], core_ids=[0])
    return r.results[0]["out"].reshape(SEQS, QLEN, D)
```
